# Optimizing a Trainium2 kernel written in Bass

```python
import numpy as np
import jax
import jax.numpy as jnp

def _softmax(x, axis=-1):
    return jax.nn.softmax(x, axis=axis)

def _gelu(x):
    return jax.nn.gelu(x, approximate=True)

def _silu(x):
    return jax.nn.silu(x)

def _sigmoid(x):
    return jax.nn.sigmoid(x)

def _layernorm(x, axis=-1, eps=1e-05):
    m = jnp.mean(x, axis=axis, keepdims=True)
    v = jnp.var(x, axis=axis, keepdims=True)
    return (x - m) / jnp.sqrt(v + eps)

def _scatter_add(tgt, idx, src, axis=0):
    return tgt.at[idx].add(src)

def _segment_sum(src, seg, n):
    return jax.ops.segment_sum(src, seg, n)
kernel_name = 'mk_adj_resnorm_d2_adj_r2_380c8d'

def setup_inputs(seed: int=0):
    np.random.seed(seed)
    _w = jnp.asarray

    def _rec_inputs():
        import jax
        import jax.numpy as jnp
        _gk = jax.random.key(seed)
        x = -0.0004776 + 1.001 * jax.random.normal(jax.random.fold_in(_gk, 1), (2048, 512), jnp.float32)
        _a = jax.random.bernoulli(jax.random.fold_in(_gk, 2), 0.00195312, (2048, 2048))
        _a = jnp.logical_or(_a, jnp.eye(2048, dtype=bool))
        _af = _a.astype(jnp.float32)
        adj = _af
        return (x, adj)
    x, adj = _rec_inputs()

    def _L0_gnn_setup():
        import jax, jax.numpy as jnp
        import numpy as np
        N, H, E, HEADS = (1500, 512, 10000, 8)
        DK = H // HEADS
        key = jax.random.key(seed)
        k1, k2, k3, k4 = jax.random.split(key, 4)
        inst_feature = jax.random.normal(k1, (N, H), dtype=jnp.float32)
        rel_pair_index = jax.random.randint(k2, (E, 2), 0, N, dtype=jnp.int64)
        agg = jnp.zeros((N, N), dtype=jnp.float32)
        agg = agg.at[rel_pair_index[:, 0], rel_pair_index[:, 1]].set(1.0)
        agg = agg.at[jnp.arange(N), jnp.arange(N)].set(1.0)
        std = float(np.sqrt(2.0 / (H + DK)))
        Wq = jax.random.normal(k3, (H, H), dtype=jnp.float32) * std
        Wk = jax.random.normal(k4, (H, H), dtype=jnp.float32) * std
        bq = jnp.zeros((H,), dtype=jnp.float32)
        bk = jnp.zeros((H,), dtype=jnp.float32)
        return {'inst_feature': inst_feature, 'aggregator_matrix': agg, 'rel_pair_index': rel_pair_index, 'Wq': Wq, 'bq': bq, 'Wk': Wk, 'bk': bk}
    _L0_gnn_all = _L0_gnn_setup()
    _L0_gnn_in = {k: v for k, v in _L0_gnn_all.items() if k in ('rel_pair_index', 'Wq', 'bq', 'Wk', 'bk')}
    del _L0_gnn_all

    def _L1_gnn_setup():
        import jax, jax.numpy as jnp
        import numpy as np
        N = 2048
        D_IN = 512
        H = 16
        DH = D_IN // H
        ALPHA = 0.2
        MASK_VAL = -65500.0
        key = jax.random.key(seed)
        ks = jax.random.split(key, 7)
        x = jax.random.normal(ks[0], (N, D_IN), dtype=jnp.float32)
        adj = jax.random.randint(ks[1], (N, N), 0, 2).astype(jnp.float32)
        s = 1.0 / np.sqrt(D_IN)
        W_seq = jax.random.normal(ks[2], (D_IN, D_IN), dtype=jnp.float32) * s
        a1 = jax.random.normal(ks[3], (DH,), dtype=jnp.float32) / np.sqrt(DH)
        a2 = jax.random.normal(ks[4], (DH,), dtype=jnp.float32) / np.sqrt(DH)
        W_out = jax.random.normal(ks[5], (D_IN, D_IN), dtype=jnp.float32) * s
        b_out = jax.random.normal(ks[6], (D_IN,), dtype=jnp.float32) * 0.01
        return {'x': x, 'adj': adj, 'W_seq': W_seq, 'a1': a1, 'a2': a2, 'W_out': W_out, 'b_out': b_out}
    _L1_gnn_all = _L1_gnn_setup()
    _L1_gnn_in = {k: v for k, v in _L1_gnn_all.items() if k in ('W_seq', 'a1', 'a2', 'W_out', 'b_out')}
    del _L1_gnn_all
    return {'x': x, 'adj': adj, 'L0_gnn_rel_pair_index': _L0_gnn_in['rel_pair_index'], 'L0_gnn_Wq': _L0_gnn_in['Wq'], 'L0_gnn_bq': _L0_gnn_in['bq'], 'L0_gnn_Wk': _L0_gnn_in['Wk'], 'L0_gnn_bk': _L0_gnn_in['bk'], 'L1_gnn_W_seq': _L1_gnn_in['W_seq'], 'L1_gnn_a1': _L1_gnn_in['a1'], 'L1_gnn_a2': _L1_gnn_in['a2'], 'L1_gnn_W_out': _L1_gnn_in['W_out'], 'L1_gnn_b_out': _L1_gnn_in['b_out']}

def reference(x, adj, L0_gnn_rel_pair_index, L0_gnn_Wq, L0_gnn_bq, L0_gnn_Wk, L0_gnn_bk, L1_gnn_W_seq, L1_gnn_a1, L1_gnn_a2, L1_gnn_W_out, L1_gnn_b_out):
    import jax
    import jax.numpy as jnp

    def _L0_gnn_ref(inst_feature, aggregator_matrix, rel_pair_index, Wq, bq, Wk, bk):
        import jax, jax.numpy as jnp
        import numpy as np
        N, H, E, HEADS = (1500, 512, 10000, 8)
        DK = H // HEADS
        n = inst_feature.shape[0]
        sub = rel_pair_index[:, 0]
        obj = rel_pair_index[:, 1]
        q = (inst_feature[sub] @ Wq.T + bq).reshape(-1, HEADS, DK)
        k = (inst_feature[obj] @ Wk.T + bk).reshape(-1, HEADS, DK)
        att = ((q * k).sum(-1) / np.sqrt(DK)).T.astype(inst_feature.dtype)
        scores = jnp.zeros((HEADS, n, n), dtype=inst_feature.dtype)
        scores = scores.at[:, sub, obj].set(att)
        mask = (1.0 - aggregator_matrix).astype(bool)
        scores = jnp.where(mask[None], -jnp.inf, scores)
        di = jnp.arange(n)
        scores = scores.at[:, di, di].set(1e-07)
        attn = jax.nn.softmax(scores, axis=2)
        aggregator_factor = attn.sum(axis=0) / HEADS
        return aggregator_factor @ inst_feature

    def _L1_gnn_ref(x, adj, W_seq, a1, a2, W_out, b_out):
        import jax, jax.numpy as jnp
        import numpy as np
        N = 2048
        D_IN = 512
        H = 16
        DH = D_IN // H
        ALPHA = 0.2
        MASK_VAL = -65500.0
        seq = (x @ W_seq).reshape(N, H, DH)
        score1 = jnp.einsum('nhd,d->hn', seq, a1)
        score2 = jnp.einsum('nhd,d->hn', seq, a2)
        scores = score1[:, :, None] + score2[:, None, :]
        scores = jax.nn.leaky_relu(scores, negative_slope=ALPHA)
        scores = scores + (1.0 - adj)[None, :, :] * MASK_VAL
        attn = jax.nn.softmax(scores, axis=-1)
        hidden = jnp.einsum('hij,jhd->ihd', attn, seq).reshape(N, D_IN)
        hidden = hidden @ W_out + b_out
        return jax.nn.elu(hidden)
    x = _layernorm(x + _L0_gnn_ref(x, adj, L0_gnn_rel_pair_index, L0_gnn_Wq, L0_gnn_bq, L0_gnn_Wk, L0_gnn_bk), axis=-1)
    x = _layernorm(x + _L1_gnn_ref(x, adj, L1_gnn_W_seq, L1_gnn_a1, L1_gnn_a2, L1_gnn_W_out, L1_gnn_b_out), axis=-1)
    return x

_drawn_inputs = setup_inputs


def setup_inputs(seed=0):
    import zlib

    import numpy as np

    out = dict(_drawn_inputs(seed))
    spreads = {'L0_gnn_bq': (0.0, 2.0), 'L0_gnn_bk': (0.0, 2.0)}
    factors = {'L0_gnn_Wq': 54.134, 'L0_gnn_Wk': 74.306, 'L1_gnn_b_out': 7.141}
    for name, (base, spread) in spreads.items():
        noise = np.random.default_rng([zlib.crc32(name.encode()), seed]).standard_normal(out[name].shape)
        drawn = base * np.exp(spread * noise) if base else spread * noise
        out[name] = jnp.asarray(drawn.astype(out[name].dtype))
    for name, factor in factors.items():
        out[name] = (out[name] * factor).astype(out[name].dtype)
    return out
```

```python
from contextlib import ExitStack

import concourse.bass as bass
from concourse import mybir

ALU = mybir.AluOpType
ACT = mybir.ActivationFunctionType
X = mybir.AxisListType.X
F32 = mybir.dt.float32
F16 = mybir.dt.float16
BF16 = mybir.dt.bfloat16
I32 = mybir.dt.int32

P = 128


class Stage:

    def __init__(self, sem, steps):
        self.sem, self.n, self.at = sem, len(steps), {s: i for i, s in enumerate(steps)}

    def after(self, turn, step):
        return turn * self.n + (self.at[step] + 1)


def two_layer_graph_attention(nc, x, adj, pairs, Wq, bq, Wk, bk, W_seq, a1, a2, W_out, b_out, out):
    N, D = x.shape
    E = pairs.shape[0]
    NB = N // P
    KT = D // P
    H0, H1 = 8, 16
    D0, D1 = D // H0, D // H1
    SLOPE, EPS, SELF = 0.2, 1e-5, 1e-7
    TC = E // P
    TAIL = E - TC * P
    T = TC + 1
    CH = 8
    FAR = 5.0e6
    assert N * N < FAR < 2 ** 23

    with ExitStack() as ctx:
        def sb(name, shape, dt=F32):
            return ctx.enter_context(nc.sbuf_tensor(name, shape, dt))

        def sem(name):
            return ctx.enter_context(nc.semaphore(name))

        def part(buf, off, shape, dt=F32):
            n = 1
            for s in shape:
                n *= s
            words = n * (2 if dt in (F16, BF16) else 4) // 4
            ap = buf[:, off:off + words]
            if dt != F32:
                ap = ap.bitcast(dt)
            names = " ".join(f"a{i}" for i in range(len(shape)))
            return ap.rearrange(f"p ({names}) -> p {names}", **{f"a{i}": s for i, s in enumerate(shape[:-1])}) \
                if len(shape) > 1 else ap

        adjT = sb("adjT", [P, NB, N], BF16)
        arenaA = sb("arenaA", [P, NB * D])
        arenaB = sb("arenaB", [P, NB * D])
        arenaC = sb("arenaC", [P, NB * D])
        stage = sb("stage", [P, 2 * N])
        ident = sb("ident", [P, P])
        ones = sb("ones", [P, P])
        before = sb("before", [P, P])
        below = sb("below", [P, P])
        iota = sb("iota", [P, N], mybir.dt.int16)
        rowid = sb("rowid", [P, NB])
        rec = sb("rec", [P, T, 16])
        recS = sb("recS", [P, T, 9])
        ohot = sb("ohot", [P, 2, CH, P], F16)
        pr = sb("pr", [P, T, 2], I32)
        prf = sb("prf", [P, T, 2])
        prh = sb("prh", [P, T, 2], F16)
        aidx = sb("aidx", [P, T], I32)
        avals = sb("avals", [P, T])
        scan = sb("scan", [P, 2, T])
        pos = sb("pos", [P, T])
        gid = sb("gid", [P, 1])
        nval = sb("nval", [P, 2])
        nvali = sb("nvali", [P, 1], I32)
        cur = sb("cur", [P, 16])
        attv = sb("attv", [P, 3, H0])
        tmp = sb("tmp", [P, 16])
        gate = sb("gate", [P, 4])
        curi = sb("curi", [P, 2], I32)
        cidx = sb("cidx", [P, 1], I32)
        winner = sb("winner", [P, 1])
        bqk = sb("bqk", [1, 2, D])
        mrow = sb("mrow", [P, NB, H0])
        cand = sb("cand", [P, NB, H0])
        racc = sb("racc", [P, NB, 9])
        deg = sb("deg", [P, 2, NB])
        rowsrc = sb("rowsrc", [P, 10])
        curS = sb("curS", [P, 9])
        rt = sb("rt", [P, 4, NB, H0])
        tab = sb("tab", [P, NB, 9])
        selfw = sb("selfw", [P, 2, NB])
        mg = sb("mg", [P, H0])
        tg = sb("tg", [P, 9])
        wv = sb("wv", [P, 4])
        bias = sb("bias", [P, 2])
        stats = sb("stats", [P, NB, 6])
        mv = sb("mv", [P, NB, 2])
        rstd = sb("rstd", [P, 2, NB])
        ps = ctx.enter_context(nc.psum_tensor("ps", [P, 8, 512], F32))

        x_in = part(arenaA, 0, [NB, D])
        WT = part(arenaA, 0, [2, KT, D])
        wide = part(arenaA, 4096, [N])
        xso = part(arenaA, 6144, [2, D])
        xsoT = part(arenaA, 7168, [2, KT, P])
        xsplit = part(arenaB, 0, [2, NB, D], F16)
        x_again = part(arenaB, 0, [NB, D])
        Wraw = part(arenaC, 4096, [2, KT, D])
        ax = part(arenaC, 0, [NB, D])
        arow = part(stage, 0, [2, N])
        prod8 = part(stage, 0, [2, H0, P])
        prod = part(stage, 0, [D])
        ksb = part(stage, 2048, [D])
        diag = part(stage, 2560, [10, P])

        owner = nc.dram_tensor("owner", (N * N, 1), F32).ap()
        mtab = nc.dram_tensor("mtab", (N, H0), F32).ap()
        wtab = nc.dram_tensor("wtab", (N, 9), F32).ap()
        etab = nc.dram_tensor("etab", (2, H1, N), F32).ap()

        adj_flat = adj.rearrange("a (b o) -> (a b) o", o=1)

        c_pr, c_x, c_w, c_b = sem("c_pr"), sem("c_x"), sem("c_w"), sem("c_b")
        c_row = [sem("c_row0"), sem("c_row1")]
        c_av = sem("c_av")
        masks, cleared, idx_made = sem("masks"), sem("cleared"), sem("idx_made")
        high_done, low_done = sem("high_done"), sem("low_done")
        turned, evac_d, evac_a = sem("turned"), sem("evac_d"), sem("evac_a")
        row_summed, row_diag = sem("row_summed"), sem("row_diag")
        ax_made, ax_saved = sem("ax_made"), sem("ax_saved")
        link_d = sem("link_d")
        tot_made, off_made, nv_made = sem("tot_made"), sem("off_made"), sem("nv_made")
        a_gather, a_scatter = sem("a_gather"), sem("a_scatter")
        m_made, m_store, b_own, b_m = sem("m_made"), sem("m_store"), sem("b_own"), sem("b_m")
        w_made, w_store, c_gather = sem("w_made"), sem("w_store"), sem("c_gather")
        mx_made, e_made, again, scaled, sw_made = (sem(n) for n in ("mx_made", "e_made", "again", "scaled", "sw_made"))
        var_made, root_made, x1_made = sem("var_made"), sem("root_made"), sem("x1_made")
        l1_load, wa_made = sem("l1_load"), sem("wa_made")
        x_turned, x_evac, seq_made, seq_saved = (sem(n) for n in ("x_turned", "x_evac", "seq_made", "seq_saved"))
        s1_turned, s1_saved, s1_store = sem("s1_turned"), sem("s1_saved"), sem("s1_store")
        g_part, g_turned, g_diag, g_all = sem("g_part"), sem("g_turned"), sem("g_diag"), sem("g_all")
        args_made, exps_made = sem("args_made"), sem("exps_made")
        c_s1 = [sem("c_s1_0"), sem("c_s1_1")]
        y_made, o_link = sem("y_made"), sem("o_link")
        o_load, h_turned, h_evac, z_made, z_neg, z_exp, z_used = (
            sem(n) for n in ("o_load", "h_turned", "h_evac", "z_made", "z_neg", "z_exp", "z_used"))
        fin, stored = sem("fin"), sem("stored")

        NCH = -(-T // CH)
        A_dve = Stage(sem("A_dve"), [f"hot{c}" for c in range(NCH)] + ["shift", "so", "idx", "prod", "red", "att",
                      "src", "attp", "diag", "eqs", "both", "any", "first", "keep", "code", "far", "mask", "back",
                      "gidc", "eq16"] + [f"{k}{b}" for b in range(NB) for k in ("mul", "max")]
                      + ["mrow", "rec", "gid", "end"])
        A_pe = Stage(sem("A_pe"), [f"list{c}" for c in range(NCH)] + ["turn", "qk", "rows"])
        A_act = Stage(sem("A_act"), ["xT0", "xT1", "k"])
        B_dve = Stage(sem("B_dve"), ["cur", "idx", "hot", "mx", "d", "cap", "S", "one", "rec",
                                     "add", "end"])
        B_pe = Stage(sem("B_pe"), ["sum"])
        B_act = Stage(sem("B_act"), ["exp"])
        C_dve = Stage(sem("C_dve"), ["cur", "curS", "idx", "hot", "sp", "g", "nb", "w", "wx"]
                      + [f"add{b}" for b in range(NB)] + ["end"])
        C_pe = Stage(sem("C_pe"), [f"corr{b}" for b in range(NB)])
        A_pool = Stage(sem("A_pool"), ["first"])
        O1_pool = Stage(sem("O1_pool"), ["first"])
        O2_pool = Stage(sem("O2_pool"), ["first"])
        O1_dve = Stage(sem("O1_dve"), ["cur", "cidx", "end"])
        O2_dve = Stage(sem("O2_dve"), ["cur", "cidx", "blank", "keep", "rec", "end"])
        owner_zero, owner_clear = sem("owner_zero"), sem("owner_clear")
        B_pool = Stage(sem("B_pool"), ["first"])
        C_pool = Stage(sem("C_pool"), ["first"])
        L_dve = Stage(sem("L_dve"), ["seqh", "Fh"] + [f"{k}{j}" for j in range(NB) for k in ("t1_", "t2_", "p_")]
                      + ["rd", "hid", "end"])
        L_pe = Stage(sem("L_pe"), [f"j{j}" for j in range(NB)])
        c_eb = sem("c_eb")

        def tiles(eng, body, count):
            body(0)
            with eng.If(P < count):
                with eng.Fori(1, T) as u:
                    with eng.If(u * P < count):
                        body(u)

        def every_tile(eng, body, count):
            with eng.Fori(0, T) as u:
                with eng.If(u * P < count):
                    body(u)

        def how_many(eng):
            eng.wait_ge(nv_made, 1)
            return eng.value_load(nvali[0:1, 0:1], min_val=0, max_val=T * P)

        def bank(n, width=512):
            return ps[:, n, 0:width]

        RB = ps[:, 5:8, :].rearrange("p a b -> p (a b)")[:, 0:10 * P].rearrange("p (r e) -> p r e", r=10)
        NW = 2 * KT
        NG = NW + NB * KT

        def evac_count(g):
            return g // 2 + 1

        def group_out(g):
            if g < NW:
                return WT[:, g // KT, g % KT, :]
            b, q = divmod(g - NW, KT)
            return adjT[:, 4 * q:4 * q + 4, b * P:(b + 1) * P]

        def group_in(g):
            return bank(g % 4) if g < NW else bank(g % 4).rearrange("p (j i) -> p j i", j=4)

        seq = part(arenaA, 0, [NB, D])
        hid = seq
        x1 = ax
        Wseq = part(stage, 0, [KT, D])
        Wa = part(stage, 2048, [KT, 2, H1])
        xT = part(stage, 2304, [2, KT, P])
        wtmp = part(arenaA, 0, [KT, H1, D1])
        eT = part(arenaB, 0, [2, N])
        p_raw = part(arenaB, 0, [N])
        p_buf = part(arenaB, N, [2, N])
        seqh = part(arenaB, 3 * N, [NB, D1 + 1])
        eB = part(stage, 0, [2, N])
        recw = rec[:].rearrange("p t r -> p (t r)")
        s12 = part(recw, 0, [NB, 2, H1])
        Fh = sb("Fh", [P, 2, NB])
        rden = sb("rden", [P, 2, 8])
        a12 = sb("a12", [P, 2, D1])
        gm = sb("gm", [P, 3, H1])
        M2 = sb("M2", [P, H1])
        EF = part(arenaB, 3 * N + NB * (D1 + 1), [4, NB, H1])
        z = part(recw, NB * 2 * H1, [2, NB, H1])
        Wo = part(stage, 0, [KT, D])
        hT = part(stage, 2048, [2, KT, P])
        zt = part(arenaB, 0, [2, D])
        ze = part(arenaB, 1024, [2, D])
        zt2 = part(arenaB, 2048, [2, D])
        bo = bqk

        block = ctx.enter_context(nc.Block())

        @block.sync
        def _(sp):
            sp.wait_ge(cleared, 1)
            sp.dma_start(pr[:, 0:TC, :], pairs[0:TC * P, :].rearrange("(p t) c -> p t c", p=P)).then_inc(c_pr, 16)
            sp.dma_start(pr[0:TAIL, TC, :], pairs[TC * P:E, :]).then_inc(c_pr, 16)
            sp.dma_start(Wraw[:, 0], Wq.rearrange("(b p) d -> p b d", p=P)).then_inc(c_w, 16)
            sp.dma_start(Wraw[:, 1], Wk.rearrange("(b p) d -> p b d", p=P)).then_inc(c_w, 16)
            sp.dma_start(x_in, x.rearrange("(b p) d -> p b d", p=P)).then_inc(c_x, 16)
            sp.dma_start(bqk[:, 0, :], bq.rearrange("(o d) -> o d", o=1)).then_inc(c_b, 16)
            sp.dma_start(bqk[:, 1, :], bk.rearrange("(o d) -> o d", o=1)).then_inc(c_b, 16)
            for b in range(NB):
                if b >= 2:
                    sp.wait_ge(turned, NW + KT * (b - 1))
                    sp.wait_ge(row_summed, b - 1)
                    sp.wait_ge(row_diag, b - 1)
                sp.dma_start(arow[:, b % 2, :], adj[b * P:(b + 1) * P, :]).then_inc(c_row[b % 2], 16)
            sp.wait_ge(ax_made, NB)
            sp.dma_start(x_again, x.rearrange("(b p) d -> p b d", p=P)).then_inc(again, 16)
            sp.dma_start(a12[:, 0, :], a1.rearrange("(o d) -> o d", o=1).to_broadcast([P, D1])).then_inc(l1_load, 16)
            sp.dma_start(a12[:, 1, :], a2.rearrange("(o d) -> o d", o=1).to_broadcast([P, D1])).then_inc(l1_load, 16)
            sp.wait_ge(m_made, 1)
            count = how_many(sp)
            with sp.If(P < count):
                sp.wait_ge(owner_zero, 1)
                for b in range(NB):
                    sp.dma_start(owner.rearrange("(b p m) o -> b p (m o)", b=NB, p=P)[b], wide).then_inc(owner_clear, 16)
            sp.dma_start(mtab.rearrange("(b p) h -> p b h", p=P), mrow[:]).then_inc(m_store, 16)
            sp.dma_start(Wseq, W_seq.rearrange("(b p) d -> p b d", p=P)).then_inc(l1_load, 16)
            sp.dma_start(bo[:, 0, :], b_out.rearrange("(o d) -> o d", o=1)).then_inc(l1_load, 16)
            sp.wait_ge(w_made, 1)
            sp.dma_start(wtab.rearrange("(b p) h -> p b h", p=P), tab[:]).then_inc(w_store, 16)
            sp.wait_ge(s1_saved, 2)
            for k in range(2):
                sp.dma_start(etab[k], eT[0:H1, k, :]).then_inc(s1_store, 16)
            sp.wait_ge(s1_store, 32)
            sp.wait_ge(seq_made, NB)
            sp.wait_ge(x_evac, NB)
            sp.dma_start(eB[:, 0, :], etab[0, 0:1, :].to_broadcast([P, N])).then_inc(c_eb, 16)
            sp.dma_start(eB[:, 1, :], etab[1, 0:1, :].to_broadcast([P, N])).then_inc(c_eb, 16)
            with sp.Fori(1, H1) as h:
                sp.wait_ge(L_dve.sem, L_dve.after(h - 1, f"t2_{NB - 1}"))
                sp.dma_start(eB[:, 0, :], etab[0, bass.ds(h, 1), :].to_broadcast([P, N])).then_inc(c_eb, 16)
                sp.dma_start(eB[:, 1, :], etab[1, bass.ds(h, 1), :].to_broadcast([P, N])).then_inc(c_eb, 16)
            sp.wait_ge(L_dve.sem, L_dve.n * H1)
            sp.dma_start(Wo, W_out.rearrange("(b p) d -> p b d", p=P)).then_inc(o_load, 16)
            for b in range(NB):
                sp.wait_ge(fin, b + 1)
                sp.dma_start(out[b * P:(b + 1) * P, :], x1[:, b, :]).then_inc(stored, 16)
            sp.wait_ge(stored, 16 * NB)

        @block.gpsimd
        def _(pool):
            g = nc.gpsimd
            g.memset(ident[:], 0.0).then_inc(masks, 1)
            g.memset(ones[:], 1.0).then_inc(masks, 1)
            g.memset(bias[:, 0:1], SELF).then_inc(masks, 1)
            g.memset(bias[:, 1:2], EPS).then_inc(masks, 1)
            g.iota(iota[:], [[1, N]], base=0, channel_multiplier=0).then_inc(masks, 1)
            g.iota(rowid[:], [[P, NB]], base=0, channel_multiplier=1,
                   allow_small_or_imprecise_dtypes=True).then_inc(masks, 1)
            g.iota(gid[:], [[1, 1]], base=0, channel_multiplier=1,
                   allow_small_or_imprecise_dtypes=True).then_inc(masks, 1)
            pool.wait_ge(masks, 7)
            g.affine_select(out=ident[:], in_=ident[:], compare_op=ALU.not_equal, fill=1.0, base=0,
                            pattern=[[-1, P]], channel_multiplier=1).then_inc(masks, 1)
            g.affine_select(out=before[:], in_=ones[:], compare_op=ALU.is_gt, fill=0.0, base=0,
                            pattern=[[-1, P]], channel_multiplier=1).then_inc(masks, 1)
            g.affine_select(out=below[:], in_=ones[:], compare_op=ALU.is_gt, fill=0.0, base=0,
                            pattern=[[1, P]], channel_multiplier=-1).then_inc(masks, 1)
            pool.wait_ge(idx_made, 1)
            for t in range(T):
                g.indirect_dma_start(out=avals[:, t:t + 1], out_offset=None, in_=adj_flat,
                                     in_offset=bass.IndirectOffsetOnAxis(ap=aidx[:, t:t + 1], axis=0)
                                     ).then_inc(c_av, 16)
            count = None

            def pass_gate(k, stage, step):
                g.tensor_tensor(gate[:, k:k + 1], ones[:, 0:1], ones[:, 1:2], ALU.mult).then_inc(stage.sem, 1)

            def loop_a(u):
                pool.wait_ge(A_dve.sem, A_dve.after(u, "idx"))
                pass_gate(0, A_pool, "first")
                for w, src in ((0, x), (1, x)):
                    g.indirect_dma_start(out=xso[:, w, :], out_offset=None, in_=src,
                                         in_offset=bass.IndirectOffsetOnAxis(ap=curi[:, w:w + 1], axis=0)
                                         ).then_inc(a_gather, 16)

            def loop_put(u):
                pool.wait_ge(O1_dve.sem, O1_dve.after(u, "cidx"))
                pass_gate(1, O1_pool, "first")
                g.indirect_dma_start(out=owner, out_offset=bass.IndirectOffsetOnAxis(ap=cidx[:, 0:1], axis=0),
                                     in_=cur[:, 11:12], in_offset=None, bounds_check=N * N - 1,
                                     oob_is_err=False).then_inc(a_scatter, 16)

            def loop_get(u):
                pool.wait_ge(O2_dve.sem, O2_dve.after(u, "blank"))
                pass_gate(2, O2_pool, "first")
                g.indirect_dma_start(out=winner[:], out_offset=None, in_=owner,
                                     in_offset=bass.IndirectOffsetOnAxis(ap=cidx[:, 0:1], axis=0),
                                     bounds_check=N * N - 1, oob_is_err=False).then_inc(b_own, 16)

            def loop_b(u):
                pool.wait_ge(B_dve.sem, B_dve.after(u, "idx"))
                pass_gate(2, B_pool, "first")
                g.indirect_dma_start(out=mg[:], out_offset=None, in_=mtab,
                                     in_offset=bass.IndirectOffsetOnAxis(ap=curi[:, 0:1], axis=0)).then_inc(b_m, 16)

            def loop_c(u):
                pool.wait_ge(C_dve.sem, C_dve.after(u, "idx"))
                pass_gate(3, C_pool, "first")
                g.indirect_dma_start(out=xso[:, 1, :], out_offset=None, in_=x,
                                     in_offset=bass.IndirectOffsetOnAxis(ap=curi[:, 1:2], axis=0)
                                     ).then_inc(c_gather, 16)
                g.indirect_dma_start(out=tg[:], out_offset=None, in_=wtab,
                                     in_offset=bass.IndirectOffsetOnAxis(ap=curi[:, 0:1], axis=0)
                                     ).then_inc(c_gather, 16)

            count = how_many(pool)
            tiles(pool, loop_a, count)
            with pool.If(P < count):
                pool.wait_ge(owner_clear, 16 * NB)
                every_tile(pool, loop_put, count)
                every_tile(pool, loop_get, count)
            pool.wait_ge(m_store, 16)
            tiles(pool, loop_b, count)
            pool.wait_ge(w_store, 16)
            tiles(pool, loop_c, count)


        @block.tensor
        def _(pe):
            t = nc.tensor
            pe.wait_ge(masks, 10)

            def turn_group(g):
                if g >= 4:
                    pe.wait_ge(evac_a if g % 2 else evac_d, evac_count(g - 4))
                for n in range(4):
                    if g < NW:
                        src = Wraw[:, g // KT, n, (g % KT) * P:(g % KT + 1) * P]
                    else:
                        b, q = divmod(g - NW, KT)
                        src = arow[:, b % 2, (4 * q + n) * P:(4 * q + n + 1) * P]
                    ins = t.transpose(bank(g % 4)[:, n * P:(n + 1) * P], src, ident[:])
                ins.then_inc(turned, 1)

            def multiply(b):
                last = NW + KT * b + KT - 1
                pe.wait_ge(evac_a, evac_count(last))
                pe.wait_ge(evac_d, evac_count(last - 1))
                if b >= 2:
                    pe.wait_ge(ax_saved, b - 1)
                for j in range(NB):
                    for w in range(2):
                        ins = t.matmul(bank(4 + b % 2), adjT[:, j, b * P:(b + 1) * P], xsplit[:, w, j, :],
                                       start=(j == 0 and w == 0), stop=(j == NB - 1 and w == 1))
                ins.then_inc(ax_made, 1)

            pe.wait_ge(c_w, 32)
            pe.wait_ge(low_done, NB)
            for g in range(NW):
                turn_group(g)
            for b in range(NB + 1):
                if b < NB:
                    pe.wait_ge(c_row[b % 2], 16 * (b // 2 + 1))
                    for q in range(KT):
                        turn_group(NW + KT * b + q)
                if b >= 1:
                    multiply(b - 1)

            pe.wait_ge(tot_made, 1)
            t.matmul(ps[:, 6, 0:1], below[:], nval[:, 0:1], start=True, stop=True)
            t.matmul(ps[:, 6, 1:2], ones[:], nval[:, 0:1], start=True, stop=True).then_inc(off_made, 1)

            def loop_a(u):
                D_, M_, S_ = A_dve, A_pe, A_act
                for c in range(NCH):
                    pe.wait_ge(D_.sem, D_.after(u, f"hot{c}"))
                    for tt in range(c * CH, min(T, (c + 1) * CH)):
                        ins = t.matmul(ps[:, 0, 0:2], ohot[:, c % 2, tt - c * CH, :], prh[:, tt, :],
                                       start=(tt == 0), stop=(tt == T - 1))
                    ins.then_inc(M_.sem, 1)
                pe.wait_ge(a_gather, 32 * (u + 1))
                for w in range(2):
                    for k in range(KT):
                        ins = t.transpose(ps[:, 1 + w, k * P:(k + 1) * P], xso[:, w, k * P:(k + 1) * P], ident[:])
                ins.then_inc(M_.sem, 1)
                pe.wait_ge(S_.sem, S_.after(u, "xT1"))
                for w in range(2):
                    for k in range(KT):
                        t.matmul(bank(3 + w), xsoT[:, w, k, :], WT[:, w, k, :], start=(k == 0), stop=False)
                    ins = t.matmul(bank(3 + w), ones[0:1, :], bqk[0:1, w, :], start=False, stop=True)
                ins.then_inc(M_.sem, 1)
                pe.wait_ge(D_.sem, D_.after(u, "diag"))
                flat = diag.rearrange("p r e -> p (r e)")
                for k in range(0, 10 * P, 512):
                    n = min(512, 10 * P - k)
                    ins = t.matmul(ps[:, 5 + k // 512, 0:n], ones[:], flat[:, k:k + n], start=True, stop=True)
                ins.then_inc(M_.sem, 1)

            def loop_b(u):
                pe.wait_ge(B_dve.sem, B_dve.after(u, "rec"))
                for b in range(NB):
                    ins = t.matmul(ps[:, 0, b * 9:(b + 1) * 9], wide[:, b * P:(b + 1) * P], curS[:],
                                   start=True, stop=True)
                ins.then_inc(B_pe.sem, 1)

            def loop_c(u):
                pe.wait_ge(C_dve.sem, C_dve.after(u, "wx"))
                for b in range(NB):
                    if b >= 8:
                        pe.wait_ge(C_dve.sem, C_dve.after(u, f"add{b - 8}"))
                    t.matmul(bank(b % 8), wide[:, b * P:(b + 1) * P], xso[:, 0, :],
                             start=True, stop=True).then_inc(C_pe.sem, 1)

            count = how_many(pe)
            pe.wait_ge(c_b, 32)
            tiles(pe, loop_a, count)
            tiles(pe, loop_b, count)
            tiles(pe, loop_c, count)

            pe.wait_ge(wa_made, 2)
            for b in range(NB):
                pe.wait_ge(x1_made, b + 1)
                if b >= 2:
                    pe.wait_ge(x_evac, b - 1)
                for k in range(KT):
                    ins = t.transpose(bank(b % 2)[:, k * P:(k + 1) * P], x1[:, b, k * P:(k + 1) * P], ident[:])
                ins.then_inc(x_turned, 1)
                pe.wait_ge(x_evac, b + 1)
                if b >= 2:
                    pe.wait_ge(seq_saved, 2 * (b - 1))
                for k in range(KT):
                    t.matmul(bank(2 + b % 2), xT[:, b % 2, k, :], Wseq[:, k, :], start=(k == 0), stop=(k == KT - 1))
                for k in range(KT):
                    ins = t.matmul(ps[:, 4 + b % 2, 0:2 * H1], xT[:, b % 2, k, :],
                                   Wa[:, k].rearrange("p s h -> p (s h)"), start=(k == 0), stop=(k == KT - 1))
                ins.then_inc(seq_made, 1)
            pe.wait_ge(g_part, 1)
            t.transpose(ps[0:H1, 6, 0:P], gm[:, 0, :], ident[:]).then_inc(g_turned, 1)
            pe.wait_ge(g_diag, 1)
            t.matmul(ps[:, 7, 0:H1], ones[0:H1, :], gm[0:H1, 1, :], start=True, stop=True).then_inc(g_all, 1)
            pe.wait_ge(exps_made, 2)
            for k in range(2):
                if k:
                    pe.wait_ge(s1_saved, 1)
                for b in range(NB):
                    ins = t.transpose(ps[0:H1, b // 4, (b % 4) * P:(b % 4 + 1) * P], EF[:, k, b, :], ident[:])
                ins.then_inc(s1_turned, 1)

            pe.wait_ge(s1_saved, 2)
            with pe.Fori(0, H1) as h:
                for j in range(NB):
                    pe.wait_ge(L_dve.sem, L_dve.after(h, f"p_{j}"))
                    for b in range(NB):
                        ins = t.matmul(ps[:, b // 8, (b % 8) * (D1 + 1):(b % 8 + 1) * (D1 + 1)],
                                       p_buf[:, j % 2, b * P:(b + 1) * P], seqh[:, j, :],
                                       start=(j == 0 and b % 8 == 0), stop=(j == NB - 1), skip_group_check=True)
                    ins.then_inc(L_pe.sem, 1)

            pe.wait_ge(o_load, 16)
            pe.wait_ge(L_dve.sem, L_dve.n * H1)
            for b in range(NB):
                if b >= 2:
                    pe.wait_ge(h_evac, b - 1)
                for k in range(KT):
                    ins = t.transpose(bank(b % 2)[:, k * P:(k + 1) * P], hid[:, b, k * P:(k + 1) * P], ident[:])
                ins.then_inc(h_turned, 1)
                pe.wait_ge(h_evac, b + 1)
                if b >= 2:
                    pe.wait_ge(z_used, b - 1)
                    pe.wait_ge(z_neg, b - 1)
                for k in range(KT):
                    t.matmul(bank(2 + b % 2), hT[:, b % 2, k, :], Wo[:, k, :], start=(k == 0), stop=False)
                t.matmul(bank(2 + b % 2), ones[0:1, :], bo[0:1, 0, :], start=False, stop=True).then_inc(z_made, 1)

        @block.scalar
        def _(act):
            s = nc.scalar
            act.wait_ge(c_x, 16)
            for b in range(NB):
                s.copy(xsplit[:, 0, b, :], x_in[:, b, :]).then_inc(high_done, 1)
            for g in range(1, NG, 2):
                act.wait_ge(turned, g + 1)
                s.copy(group_out(g), group_in(g)).then_inc(evac_a, 1)
                if g >= NW and (g - NW) % KT == 1:
                    b = (g - NW) // KT
                    if b >= 1:
                        act.wait_ge(row_summed, b)
                    s.activation(ohot[:].rearrange("p a b c -> p (a b c)")[:, 0:N], arow[:, b % 2, :], ACT.Identity,
                                 accum_out=deg[:, 0, b:b + 1]).then_inc(row_summed, 1)

            def loop_a(u):
                act.wait_ge(A_pe.sem, A_pe.after(u, "turn"))
                for w in range(2):
                    s.copy(xsoT[:, w].rearrange("p k e -> p (k e)"), bank(1 + w)).then_inc(A_act.sem, 1)
                act.wait_ge(A_pe.sem, A_pe.after(u, "qk"))
                s.copy(ksb, bank(4)).then_inc(A_act.sem, 1)

            def loop_b(u):
                act.wait_ge(B_dve.sem, B_dve.after(u, "cap"))
                s.activation(attv[:, 1, :], attv[:, 0, :], ACT.Exp).then_inc(B_act.sem, 1)

            count = how_many(act)
            tiles(act, loop_a, count)
            tiles(act, loop_b, count)
            act.wait_ge(mx_made, 1)
            s.activation(rt[:, 1], rt[:, 0], ACT.Exp, scale=-1.0).then_inc(e_made, 1)
            s.activation(rt[:, 2], rt[:, 0], ACT.Exp, scale=-1.0, bias=bias[:, 0:1]).then_inc(e_made, 1)
            act.wait_ge(var_made, NB)
            s.activation(rstd[:, 0, :], mv[:, :, 1], ACT.Sqrt, bias=bias[:, 1:2]).then_inc(root_made, 1)
            for b in range(NB):
                act.wait_ge(x_turned, b + 1)
                if b >= 2:
                    act.wait_ge(seq_made, b - 1)
                s.copy(xT[:, b % 2].rearrange("p k e -> p (k e)"), bank(b % 2)).then_inc(x_evac, 1)
            act.wait_ge(args_made, 1)
            for k in range(2):
                s.activation(EF[:, k], z[:, k], ACT.Exp).then_inc(exps_made, 1)
            act.wait_ge(args_made, 2)
            s.activation(EF[:, 2], z[:, 0], ACT.Exp).then_inc(exps_made, 1)
            s.activation(EF[:, 3], z[:, 0], ACT.Exp, scale=SLOPE).then_inc(exps_made, 1)
            for k in range(2):
                act.wait_ge(s1_turned, k + 1)
                s.copy(eT[0:H1, k, :], ps[0:H1, 0:4, :].rearrange("p a b -> p (a b)")).then_inc(s1_saved, 1)
            for b in range(NB):
                act.wait_ge(h_turned, b + 1)
                if b >= 2:
                    act.wait_ge(z_made, b - 1)
                s.copy(hT[:, b % 2].rearrange("p k e -> p (k e)"), bank(b % 2)).then_inc(h_evac, 1)
                act.wait_ge(z_made, b + 1)
                if b >= 2:
                    act.wait_ge(z_used, b - 1)
                s.activation(zt[:, b % 2, :], bank(2 + b % 2), ACT.Relu, scale=-1.0).then_inc(z_neg, 1)
                act.wait_ge(z_neg, b + 1)
                s.activation(ze[:, b % 2, :], zt[:, b % 2, :], ACT.Exp, scale=-1.0).then_inc(z_exp, 1)
            act.wait_ge(var_made, 2 * NB)
            s.activation(rstd[:, 0, :], mv[:, :, 1], ACT.Sqrt, bias=bias[:, 1:2]).then_inc(root_made, 1)

        @block.vector
        def _(dve):
            v = nc.vector
            links = [0]

            def link(ins):
                links[0] += 1
                ins.then_inc(link_d, 1)
                dve.wait_ge(link_d, links[0])

            v.memset(racc[:], 0.0)
            v.memset(mrow[:], 0.0)
            v.memset(winner[:], -1.0)
            v.memset(cur[:], 0.0)
            v.memset(pr[:], 0).then_inc(cleared, 1)
            dve.wait_ge(c_pr, 32)
            link(v.tensor_copy(prf[:], pr[:]))
            link(v.tensor_scalar_add(prh[:], prf[:], 1.0))
            v.scalar_tensor_tensor(aidx[:], prf[:, :, 0], float(N), prf[:, :, 1], ALU.mult, ALU.add).then_inc(idx_made, 1)
            for b in range(NB):
                dve.wait_ge(high_done, b + 1)
                v.tensor_tensor(xsplit[:, 1, b, :], x_in[:, b, :], xsplit[:, 0, b, :], ALU.subtract).then_inc(low_done, 1)

            def save_ax(b):
                dve.wait_ge(ax_made, b + 1)
                v.tensor_copy(ax[:, b, :], bank(4 + b % 2)).then_inc(ax_saved, 1)

            dve.wait_ge(masks, 10)
            for g in range(0, NG, 2):
                dve.wait_ge(turned, g + 1)
                v.tensor_copy(group_out(g), group_in(g)).then_inc(evac_d, 1)
                if g >= NW and (g - NW) % KT == 2:
                    b = (g - NW) // KT
                    if b >= 1:
                        dve.wait_ge(row_diag, b)
                    v.tensor_tensor_reduce(cand[:].rearrange("p b h -> p (b h)"), arow[:, b % 2, b * P:(b + 1) * P], ident[:], 1.0, 0.0,
                                           ALU.mult, ALU.add, deg[:, 1, b:b + 1]).then_inc(row_diag, 1)
                    if b >= 1:
                        save_ax(b - 1)
            save_ax(NB - 1)

            dve.wait_ge(c_av, 16 * T)
            link(v.tensor_tensor(scan[:, 0, :], prf[:, :, 0], prf[:, :, 1], ALU.not_equal))
            link(v.tensor_tensor(avals[:], avals[:], scan[:, 0, :], ALU.mult))
            link(v.tensor_copy(scan[:, 0, :], avals[:]))
            side, d = 0, 1
            while d < T:
                v.tensor_copy(scan[:, 1 - side, 0:d], scan[:, side, 0:d])
                link(v.tensor_tensor(scan[:, 1 - side, d:T], scan[:, side, d:T], scan[:, side, 0:T - d], ALU.add))
                side, d = 1 - side, 2 * d
            v.tensor_copy(nval[:, 0:1], scan[:, side, T - 1:T]).then_inc(tot_made, 1)
            dve.wait_ge(off_made, 1)
            link(v.tensor_copy(nval[:, 1:2], ps[:, 6, 0:1]))
            v.tensor_copy(nvali[:], ps[:, 6, 1:2]).then_inc(nv_made, 1)
            link(v.scalar_tensor_tensor(pos[:], scan[:, side, :], nval[:, 1:2], avals[:], ALU.add, ALU.mult))
            link(v.tensor_scalar_add(pos[:], pos[:], -1.0))

            def at(rows, u):
                return rows[:, u, :] if isinstance(u, int) else rows[:, bass.ds(u, 1), :]

            def as_slot(tile, u):
                return tile[:] if isinstance(u, int) else tile[:].unsqueeze(1)

            def loop_a(u):
                S = A_dve

                def own(step):
                    dve.wait_ge(S.sem, S.after(u, step))

                for c in range(NCH):
                    n = min(CH, T - c * CH)
                    if c >= 2:
                        dve.wait_ge(A_pe.sem, A_pe.after(u, f"list{c - 2}"))
                    v.tensor_tensor(ohot[:, c % 2, 0:n, :], pos[:, c * CH:c * CH + n].unsqueeze(2).to_broadcast([P, n, P]),
                                    iota[:, 0:P].unsqueeze(1).to_broadcast([P, n, P]), ALU.is_equal).then_inc(S.sem, 1)
                own(f"hot{NCH - 1}")
                v.tensor_scalar_add(pos[:], pos[:], -float(P)).then_inc(S.sem, 1)
                dve.wait_ge(A_pe.sem, A_pe.after(u, f"list{NCH - 1}"))
                v.tensor_scalar_add(cur[:, 0:2], ps[:, 0, 0:2], -1.0).then_inc(S.sem, 1)
                own("so")
                v.tensor_scalar_max(curi[:], cur[:, 0:2], 0.0).then_inc(S.sem, 1)
                dve.wait_ge(A_act.sem, A_act.after(u, "k"))
                v.tensor_tensor(prod, bank(3), ksb, ALU.mult).then_inc(S.sem, 1)
                own("prod")
                v.tensor_reduce(attv[:, 0, :], prod.rearrange("p (h d) -> p h d", h=H0), X, ALU.add).then_inc(S.sem, 1)
                own("red")
                v.tensor_scalar_mul(cur[:, 2:2 + H0], attv[:, 0, :], float(D0) ** -0.5).then_inc(S.sem, 1)
                own("att")
                v.tensor_copy(rowsrc[:, 0:2], cur[:, 0:2]).then_inc(S.sem, 1)
                v.tensor_scalar_max(rowsrc[:, 2:10], cur[:, 2:10], 0.0).then_inc(S.sem, 1)
                own("attp")
                v.tensor_tensor(diag, ident[:].unsqueeze(1).to_broadcast([P, 10, P]),
                                rowsrc[:].unsqueeze(2).to_broadcast([P, 10, P]), ALU.mult).then_inc(S.sem, 1)
                dve.wait_ge(A_pe.sem, A_pe.after(u, "rows"))
                e1, e2 = part(stage, 1024, [P]), part(stage, 1024 + P, [P])
                v.scalar_tensor_tensor(e1, RB[:, 0, :], cur[:, 0:1], before[:], ALU.is_equal, ALU.mult).then_inc(S.sem, 1)
                own("eqs")
                v.scalar_tensor_tensor(e2, RB[:, 1, :], cur[:, 1:2], e1, ALU.is_equal, ALU.mult).then_inc(S.sem, 1)
                own("both")
                v.tensor_reduce(tmp[:, 0:1], e2, X, ALU.max).then_inc(S.sem, 1)
                own("any")
                v.tensor_scalar(tmp[:, 1:2], tmp[:, 0:1], -1.0, 1.0, ALU.mult, ALU.add).then_inc(S.sem, 1)
                own("first")
                v.scalar_tensor_tensor(cur[:, 10:11], cur[:, 0:1], 0.0, tmp[:, 1:2], ALU.is_ge, ALU.mult).then_inc(S.sem, 1)
                own("keep")
                v.scalar_tensor_tensor(tmp[:, 2:3], cur[:, 0:1], float(N), cur[:, 1:2], ALU.mult, ALU.add).then_inc(S.sem, 1)
                own("code")
                v.tensor_scalar_add(tmp[:, 3:4], tmp[:, 2:3], -FAR).then_inc(S.sem, 1)
                own("far")
                v.tensor_tensor(tmp[:, 4:5], tmp[:, 3:4], cur[:, 10:11], ALU.mult).then_inc(S.sem, 1)
                own("mask")
                v.tensor_scalar_add(cur[:, 12:13], tmp[:, 4:5], FAR).then_inc(S.sem, 1)
                own("back")
                v.tensor_copy(cur[:, 11:12], gid[:]).then_inc(S.sem, 1)
                hot = wide.rearrange("p (b e) -> p b e", b=NB)
                v.tensor_tensor(hot, RB[:, 0, :].unsqueeze(1).to_broadcast([P, NB, P]),
                                rowid[:].unsqueeze(2).to_broadcast([P, NB, P]), ALU.is_equal).then_inc(S.sem, 1)
                own("eq16")
                for b in range(NB):
                    v.tensor_tensor(prod8[:, b % 2], RB[:, 2:10, :], hot[:, b, :].unsqueeze(1).to_broadcast([P, H0, P]),
                                    ALU.mult).then_inc(S.sem, 1)
                    own(f"mul{b}")
                    v.tensor_reduce(cand[:, b, :], prod8[:, b % 2], X, ALU.max).then_inc(S.sem, 1)
                own(f"max{NB - 1}")
                v.tensor_tensor(mrow[:], mrow[:], cand[:], ALU.max).then_inc(S.sem, 1)
                v.tensor_scalar_mul(at(rec, u), as_slot(cur, u), 1.0).then_inc(S.sem, 1)
                own("rec")
                v.tensor_scalar_add(gid[:], gid[:], float(P)).then_inc(S.sem, 1)
                own("gid")
                dve.wait_ge(A_pool.sem, A_pool.after(u, "first"))
                v.memset(wv[:, 3:4], 0.0).then_inc(S.sem, 1)

            def loop_put(u):
                S = O1_dve
                v.tensor_scalar_mul(cur[:].unsqueeze(1), rec[:, bass.ds(u, 1), :], 1.0).then_inc(S.sem, 1)
                dve.wait_ge(S.sem, S.after(u, "cur"))
                v.tensor_copy(cidx[:], cur[:, 12:13]).then_inc(S.sem, 1)
                dve.wait_ge(a_scatter, 16 * (u + 1))
                dve.wait_ge(O1_pool.sem, O1_pool.after(u, "first"))
                dve.wait_ge(S.sem, S.after(u, "cidx"))
                v.memset(wv[:, 3:4], 0.0).then_inc(S.sem, 1)

            def loop_get(u):
                S = O2_dve

                def own(step):
                    dve.wait_ge(S.sem, S.after(u, step))

                v.tensor_scalar_mul(cur[:].unsqueeze(1), rec[:, bass.ds(u, 1), :], 1.0).then_inc(S.sem, 1)
                own("cur")
                v.tensor_copy(cidx[:], cur[:, 12:13]).then_inc(S.sem, 1)
                v.memset(winner[:], -1.0).then_inc(S.sem, 1)
                own("blank")
                dve.wait_ge(O2_pool.sem, O2_pool.after(u, "first"))
                dve.wait_ge(b_own, 16 * (u + 1))
                v.scalar_tensor_tensor(cur[:, 10:11], winner[:], cur[:, 11:12], cur[:, 10:11], ALU.is_equal,
                                       ALU.mult).then_inc(S.sem, 1)
                own("keep")
                v.tensor_scalar_mul(rec[:, bass.ds(u, 1), :], cur[:].unsqueeze(1), 1.0).then_inc(S.sem, 1)
                own("rec")
                v.memset(wv[:, 3:4], 0.0).then_inc(S.sem, 1)

            def loop_b(u):
                S = B_dve

                def own(step):
                    dve.wait_ge(S.sem, S.after(u, step))

                v.tensor_scalar_mul(as_slot(cur, u), at(rec, u), 1.0).then_inc(S.sem, 1)
                own("cur")
                v.tensor_scalar_max(curi[:], cur[:, 0:2], 0.0).then_inc(S.sem, 1)
                v.tensor_scalar(wide, iota[:], cur[:, 0:1], None, ALU.is_equal).then_inc(S.sem, 1)
                own("hot")
                dve.wait_ge(b_m, 16 * (u + 1))
                dve.wait_ge(B_pool.sem, B_pool.after(u, "first"))
                v.tensor_scalar_max(mg[:], mg[:], SELF).then_inc(S.sem, 1)
                own("mx")
                v.tensor_tensor(attv[:, 2, :], cur[:, 2:10], mg[:], ALU.subtract).then_inc(S.sem, 1)
                own("d")
                v.tensor_scalar_min(attv[:, 0, :], attv[:, 2, :], 0.0).then_inc(S.sem, 1)
                dve.wait_ge(B_act.sem, B_act.after(u, "exp"))
                v.tensor_scalar(curS[:, 0:H0], attv[:, 1, :], cur[:, 10:11], None, ALU.mult).then_inc(S.sem, 1)
                v.tensor_copy(curS[:, H0:H0 + 1], cur[:, 10:11]).then_inc(S.sem, 1)
                own("one")
                v.tensor_scalar_mul(at(recS, u), as_slot(curS, u), 1.0).then_inc(S.sem, 1)
                dve.wait_ge(B_pe.sem, B_pe.after(u, "sum"))
                v.tensor_tensor(racc[:], racc[:], ps[:, 0, 0:9 * NB].rearrange("p (b k) -> p b k", b=NB),
                                ALU.add).then_inc(S.sem, 1)
                own("add")
                v.memset(wv[:, 3:4], 0.0).then_inc(S.sem, 1)

            def loop_c(u):
                S = C_dve

                def own(step):
                    dve.wait_ge(S.sem, S.after(u, step))

                v.tensor_scalar_mul(as_slot(cur, u), at(rec, u), 1.0).then_inc(S.sem, 1)
                v.tensor_scalar_mul(as_slot(curS, u), at(recS, u), 1.0).then_inc(S.sem, 1)
                own("curS")
                v.tensor_scalar_max(curi[:], cur[:, 0:2], 0.0).then_inc(S.sem, 1)
                v.tensor_scalar(wide, iota[:], cur[:, 0:1], None, ALU.is_equal).then_inc(S.sem, 1)
                dve.wait_ge(c_gather, 32 * (u + 1))
                dve.wait_ge(C_pool.sem, C_pool.after(u, "first"))
                v.tensor_tensor(attv[:, 0, :], curS[:, 0:H0], tg[:, 0:H0], ALU.mult).then_inc(S.sem, 1)
                own("sp")
                v.tensor_reduce(wv[:, 0:1], attv[:, 0, :], X, ALU.add).then_inc(S.sem, 1)
                v.tensor_tensor(wv[:, 1:2], curS[:, H0:H0 + 1], tg[:, H0:H0 + 1], ALU.mult).then_inc(S.sem, 1)
                own("nb")
                v.tensor_tensor(wv[:, 2:3], wv[:, 0:1], wv[:, 1:2], ALU.subtract).then_inc(S.sem, 1)
                own("w")
                v.tensor_scalar(xso[:, 0, :], xso[:, 1, :], wv[:, 2:3], None, ALU.mult).then_inc(S.sem, 1)
                for b in range(NB):
                    dve.wait_ge(C_pe.sem, C_pe.after(u, f"corr{b}"))
                    v.tensor_tensor(ax[:, b, :], ax[:, b, :], bank(b % 8), ALU.add).then_inc(S.sem, 1)
                own(f"add{NB - 1}")
                v.memset(wv[:, 3:4], 0.0).then_inc(S.sem, 1)

            count = how_many(dve)
            tiles(dve, loop_a, count)
            v.tensor_copy(rt[:, 3], mrow[:]).then_inc(m_made, 1)
            with dve.If(P < count):
                v.memset(wide, 0.0).then_inc(owner_zero, 1)
                every_tile(dve, loop_put, count)
                every_tile(dve, loop_get, count)
            tiles(dve, loop_b, count)

            v.tensor_scalar_max(rt[:, 0], mrow[:], SELF).then_inc(mx_made, 1)
            link(v.tensor_tensor(selfw[:, 0, :], deg[:, 0, :], deg[:, 1, :], ALU.subtract))
            link(v.tensor_tensor(selfw[:, 1, :], selfw[:, 0, :], racc[:, :, H0], ALU.subtract))
            dve.wait_ge(e_made, 2)
            link(v.tensor_tensor(rt[:, 3], rt[:, 1], selfw[:, 1, :].unsqueeze(2).to_broadcast([P, NB, H0]), ALU.mult))
            link(v.tensor_tensor(rt[:, 3], rt[:, 3], rt[:, 2], ALU.add))
            link(v.tensor_tensor(rt[:, 3], rt[:, 3], racc[:, :, 0:H0], ALU.add))
            link(v.reciprocal(rt[:, 0], rt[:, 3]))
            link(v.tensor_scalar_mul(tab[:, :, 0:H0], rt[:, 0], 1.0 / H0))
            link(v.tensor_tensor(rt[:, 3], rt[:, 1], tab[:, :, 0:H0], ALU.mult))
            v.tensor_reduce(tab[:, :, H0:H0 + 1], rt[:, 3], X, ALU.add).then_inc(w_made, 1)
            link(v.tensor_tensor(rt[:, 0], rt[:, 2], tab[:, :, 0:H0], ALU.mult))
            dve.wait_ge(w_made, 1)
            link(v.tensor_reduce(selfw[:, 0, :], rt[:, 0], X, ALU.add))
            link(v.tensor_tensor(selfw[:, 1, :], tab[:, :, H0], deg[:, 1, :], ALU.mult))
            link(v.tensor_tensor(selfw[:, 0, :], selfw[:, 0, :], selfw[:, 1, :], ALU.subtract))
            link(v.tensor_scalar_add(selfw[:, 1, :], selfw[:, 0, :], 1.0))
            dve.wait_ge(again, 16)
            for b in range(NB):
                v.tensor_scalar(x_again[:, b, :], x_again[:, b, :], selfw[:, 1, b:b + 1], None,
                                ALU.mult).then_inc(scaled, 1)
            for b in range(NB):
                dve.wait_ge(scaled, b + 1)
                link(v.scalar_tensor_tensor(ax[:, b, :], ax[:, b, :], tab[:, b, H0:H0 + 1], x_again[:, b, :],
                                            ALU.mult, ALU.add))
            tiles(dve, loop_c, count)

            def normalize(done, layer):
                for b in range(NB):
                    if layer:
                        add_elu(b)
                    link(v.bn_stats(stats[:, b, :], x1[:, b, :]))
                    v.bn_aggr(mv[:, b, :], stats[:, b, :]).then_inc(var_made, 1)
                dve.wait_ge(root_made, layer + 1)
                link(v.reciprocal(rstd[:, 1, :], rstd[:, 0, :]))
                for b in range(NB):
                    v.tensor_scalar(x1[:, b, :], x1[:, b, :], mv[:, b, 0:1], rstd[:, 1, b:b + 1], ALU.subtract,
                                    ALU.mult).then_inc(done, 1)

            def add_elu(b):
                dve.wait_ge(z_exp, b + 1)
                link(v.scalar_tensor_tensor(zt2[:, b % 2, :], bank(2 + b % 2), 0.0, ze[:, b % 2, :], ALU.max, ALU.add))
                v.scalar_tensor_tensor(x1[:, b, :], zt2[:, b % 2, :], -1.0, x1[:, b, :], ALU.add,
                                       ALU.add).then_inc(z_used, 1)
                dve.wait_ge(z_used, b + 1)

            normalize(x1_made, 0)

            dve.wait_ge(l1_load, 64)
            for k in range(2):
                link(v.tensor_tensor(wtmp.rearrange("p k h d -> p (k h) d"),
                                     Wseq.rearrange("p k (h d) -> p (k h) d", h=H1),
                                     a12[:, k, :].unsqueeze(1).to_broadcast([P, KT * H1, D1]), ALU.mult))
                v.tensor_reduce(Wa[:, :, k, :], wtmp, X, ALU.add).then_inc(wa_made, 1)
                dve.wait_ge(wa_made, k + 1)
            for b in range(NB):
                dve.wait_ge(seq_made, b + 1)
                v.tensor_copy(seq[:, b, :], bank(2 + b % 2)).then_inc(seq_saved, 1)
                v.tensor_copy(s12[:, b].rearrange("p s h -> p (s h)"), ps[:, 4 + b % 2, 0:2 * H1]).then_inc(seq_saved, 1)
            dve.wait_ge(seq_saved, 2 * NB)
            v.tensor_reduce(gm[:, 0, :], s12[:, :, 1, :].rearrange("p b h -> p h b"), X, ALU.max).then_inc(g_part, 1)
            dve.wait_ge(g_turned, 1)
            link(v.tensor_reduce(gm[0:H1, 2, 0:1], ps[0:H1, 6, 0:P], X, ALU.max))
            v.tensor_scalar(gm[0:H1, 1, :], ident[0:H1, 0:H1], gm[0:H1, 2, 0:1], None, ALU.mult).then_inc(g_diag, 1)
            dve.wait_ge(g_all, 1)
            link(v.tensor_copy(M2[:], ps[:, 7, 0:H1]))
            mB = M2[:].unsqueeze(1).to_broadcast([P, NB, H1])
            link(v.tensor_tensor(EF[:, 0], s12[:, :, 0, :], mB, ALU.add))
            link(v.scalar_tensor_tensor(EF[:, 1], EF[:, 0], SLOPE, EF[:, 0], ALU.mult, ALU.max))
            link(v.tensor_tensor(z[:, 0], EF[:, 0], EF[:, 1], ALU.subtract))
            v.scalar_tensor_tensor(z[:, 1], EF[:, 0], SLOPE, EF[:, 1], ALU.mult, ALU.subtract).then_inc(args_made, 1)
            dve.wait_ge(exps_made, 1)
            v.tensor_tensor(z[:, 0], s12[:, :, 1, :], mB, ALU.subtract).then_inc(args_made, 1)
            dve.wait_ge(exps_made, 4)
            dve.wait_ge(s1_store, 32)
            link(v.memset(seqh[:, :, D1:D1 + 1], 1.0))
            with dve.Fori(0, H1) as h:
                L = L_dve

                def own(step):
                    dve.wait_ge(L.sem, L.after(h, step))

                v.tensor_scalar_mul(seqh[:, :, 0:D1], seq[:, :, bass.ds(h * D1, D1)], 1.0).then_inc(L.sem, 1)
                v.tensor_scalar_mul(Fh[:].unsqueeze(3), EF[:, 2:4, :, bass.ds(h, 1)], 1.0).then_inc(L.sem, 1)
                own("Fh")
                dve.wait_ge(c_eb, 32 * (h + 1))
                for j in range(NB):
                    v.tensor_scalar(p_raw, eB[:, 0, :], Fh[:, 0, j:j + 1], None, ALU.mult).then_inc(L.sem, 1)
                    own(f"t1_{j}")
                    v.scalar_tensor_tensor(p_raw, eB[:, 1, :], Fh[:, 1, j:j + 1], p_raw, ALU.mult,
                                           ALU.max).then_inc(L.sem, 1)
                    own(f"t2_{j}")
                    if j >= 2:
                        dve.wait_ge(L_pe.sem, L_pe.after(h, f"j{j - 2}"))
                    v.tensor_tensor(p_buf[:, j % 2, :], p_raw, adjT[:, j, :], ALU.mult).then_inc(L.sem, 1)
                    own(f"p_{j}")
                dve.wait_ge(L_pe.sem, L_pe.after(h, f"j{NB - 1}"))
                O = ps[:, 0:2, 0:8 * (D1 + 1)].rearrange("p a (b d) -> p a b d", b=8)
                v.reciprocal(rden[:].unsqueeze(3), O[:, :, :, D1:D1 + 1]).then_inc(L.sem, 1)
                own("rd")
                for a in range(2):
                    ins = v.tensor_tensor(hid[:, 8 * a:8 * a + 8, bass.ds(h * D1, D1)], O[:, a, :, 0:D1],
                                          rden[:, a, :].unsqueeze(2).to_broadcast([P, 8, D1]), ALU.mult)
                ins.then_inc(L.sem, 1)
                own("hid")
                v.memset(wv[:, 3:4], 0.0).then_inc(L.sem, 1)
            normalize(fin, 1)


_INS = ['x', 'adj', 'L0_gnn_rel_pair_index', 'L0_gnn_Wq', 'L0_gnn_bq', 'L0_gnn_Wk', 'L0_gnn_bk', 'L1_gnn_W_seq',
        'L1_gnn_a1', 'L1_gnn_a2', 'L1_gnn_W_out', 'L1_gnn_b_out']
_OUTS = [((2048, 512), 'float32')]


def kernel(**inputs):
    import numpy as _np
    import concourse.bacc as _bacc
    from concourse import mybir as _mybir
    from concourse.bass_utils import run_bass_kernel_spmd as _run

    nc = _bacc.Bacc("TRN2", target_bir_lowering=False, num_devices=1)
    arrays, args = {}, []
    for name in _INS:
        a = _np.ascontiguousarray(inputs[name])
        arrays[f"in_{name}_dram"] = a
        args.append(nc.dram_tensor(f"in_{name}_dram", a.shape, _mybir.dt.from_np(a.dtype), kind="ExternalInput").ap())
    for i, (shape, dtype) in enumerate(_OUTS):
        dt = _mybir.dt.from_np(_np.dtype(dtype))
        args.append(nc.dram_tensor(f"out_{i}_dram", shape, dt, kind="ExternalOutput").ap())
    two_layer_graph_attention(nc, *args)
    r = _run(nc, [arrays], core_ids=[0])
    got = tuple(r.results[0][f"out_{i}_dram"] for i in range(len(_OUTS)))
    return got[0]
```

```python
from contextlib import ExitStack

import concourse.bass as bass
from concourse import mybir

ALU = mybir.AluOpType
ACT = mybir.ActivationFunctionType
X = mybir.AxisListType.X
F32 = mybir.dt.float32
F16 = mybir.dt.float16
BF16 = mybir.dt.bfloat16
I32 = mybir.dt.int32

P = 128


class Stage:

    def __init__(self, sem, steps):
        self.sem, self.n, self.at = sem, len(steps), {s: i for i, s in enumerate(steps)}

    def after(self, turn, step):
        return turn * self.n + (self.at[step] + 1)


def two_layer_graph_attention(nc, x, adj, pairs, Wq, bq, Wk, bk, W_seq, a1, a2, W_out, b_out, out):
    N, D = x.shape
    E = pairs.shape[0]
    NB = N // P
    KT = D // P
    H0, H1 = 8, 16
    D0, D1 = D // H0, D // H1
    SLOPE, EPS, SELF = 0.2, 1e-5, 1e-7
    TC = E // P
    TAIL = E - TC * P
    T = TC + 1
    CH = 8
    KE = 6
    GR = 3
    FAR = 5.0e6
    assert N * N < FAR < 2 ** 23

    with ExitStack() as ctx:
        def sb(name, shape, dt=F32):
            return ctx.enter_context(nc.sbuf_tensor(name, shape, dt))

        def sem(name):
            return ctx.enter_context(nc.semaphore(name))

        def part(buf, off, shape, dt=F32):
            n = 1
            for s in shape:
                n *= s
            words = n * (2 if dt in (F16, BF16) else 4) // 4
            ap = buf[:, off:off + words]
            if dt != F32:
                ap = ap.bitcast(dt)
            names = " ".join(f"a{i}" for i in range(len(shape)))
            return ap.rearrange(f"p ({names}) -> p {names}", **{f"a{i}": s for i, s in enumerate(shape[:-1])}) \
                if len(shape) > 1 else ap

        adjT = sb("adjT", [P, NB, N], BF16)
        arenaA = sb("arenaA", [P, NB * D])
        arenaB = sb("arenaB", [P, NB * D])
        arenaC = sb("arenaC", [P, NB * D])
        stage = sb("stage", [P, 2 * N])
        ident = sb("ident", [P, P])
        ones = sb("ones", [P, P])
        before = sb("before", [P, P])
        below = sb("below", [P, P])
        iota = sb("iota", [P, N], mybir.dt.int16)
        rowid = sb("rowid", [P, NB])
        rec = sb("rec", [P, T, 13])
        recS = sb("recS", [P, T, 9])
        ohot = sb("ohot", [P, 2, CH, P], F16)
        pr = sb("pr", [P, T, 2], I32)
        prf = sb("prf", [P, T, 2])
        prh = sb("prh", [P, T, 2], F16)
        aidx = sb("aidx", [P, T], I32)
        avals = sb("avals", [P, T])
        pos = sb("pos", [P, T])
        gid = sb("gid", [P, 1])
        nval = sb("nval", [P, 2])
        nvali = sb("nvali", [P, 1], I32)
        cur = sb("cur", [P, 13])
        attv = sb("attv", [P, 3, H0])
        tmp = sb("tmp", [P, 16])
        gate = sb("gate", [P, 4])
        curi = sb("curi", [P, 2], I32)
        cidx = sb("cidx", [P, 1], I32)
        winner = sb("winner", [P, 1])
        bqk = sb("bqk", [1, 2, D])
        mrow = sb("mrow", [P, NB, H0])
        racc = sb("racc", [P, NB, 9])
        deg = sb("deg", [P, 2, NB])
        rowsrc = sb("rowsrc", [P, 10])
        curS = sb("curS", [P, 9])
        rt = sb("rt", [P, 4, NB, H0])
        tab = sb("tab", [P, NB, 9])
        selfw = sb("selfw", [P, 2, NB])
        mg = sb("mg", [P, H0])
        tg = sb("tg", [P, 9])
        wv = sb("wv", [P, 4])
        bias = sb("bias", [P, 2])
        stats = sb("stats", [P, NB, 6])
        mv = sb("mv", [P, NB, 2])
        rstd = sb("rstd", [P, 2, NB])
        ps = ctx.enter_context(nc.psum_tensor("ps", [P, 8, 512], F32))

        x_in = part(arenaA, 0, [NB, D])
        WT = part(arenaA, 0, [2, KT, D])
        wide = part(arenaA, 4096, [N])
        xso = part(arenaA, 6144, [2, D])
        xsoT = part(arenaA, 7168, [2, KT, P])
        xsplit = part(arenaB, 0, [2, NB, D], F16)
        x_again = part(arenaB, 0, [NB, D])
        Wraw = part(arenaC, 4096, [2, KT, D])
        ax = part(arenaC, 0, [NB, D])
        arow = part(stage, 0, [2, N])
        prod8 = part(stage, 0, [H0, P])
        prod = part(stage, 0, [D])
        ksb = part(stage, 2048, [D])
        diag = part(stage, 2560, [10, P])

        owner = nc.dram_tensor("owner", (N * N, 1), F32).ap()
        mtab = nc.dram_tensor("mtab", (N, H0), F32).ap()
        wtab = nc.dram_tensor("wtab", (N, 9), F32).ap()
        seqtab = nc.dram_tensor("seqtab", (N, D + H1), F32).ap()
        etab = nc.dram_tensor("etab", (2, H1, N), F32).ap()

        adj_flat = adj.rearrange("a (b o) -> (a b) o", o=1)

        c_pr, c_x, c_w, c_b = sem("c_pr"), sem("c_x"), sem("c_w"), sem("c_b")
        c_row = [sem("c_row0"), sem("c_row1")]
        c_av = sem("c_av")
        masks, cleared, idx_made = sem("masks"), sem("cleared"), sem("idx_made")
        high_done, low_done = sem("high_done"), sem("low_done")
        turned, evac_d, evac_a = sem("turned"), sem("evac_d"), sem("evac_a")
        row_summed, row_diag = sem("row_summed"), sem("row_diag")
        ax_made, ax_saved = sem("ax_made"), sem("ax_saved")
        link_d = sem("link_d")
        tot_made, off_made, nv_made = sem("tot_made"), sem("off_made"), sem("nv_made")
        a_gather, a_scatter = sem("a_gather"), sem("a_scatter")
        m_made, m_store, b_own, b_m = sem("m_made"), sem("m_store"), sem("b_own"), sem("b_m")
        w_made, w_store, c_gather = sem("w_made"), sem("w_store"), sem("c_gather")
        mx_made, e_made, again, scaled, sw_made = (sem(n) for n in ("mx_made", "e_made", "again", "scaled", "sw_made"))
        var_made, root_made, x1_made = sem("var_made"), sem("root_made"), sem("x1_made")
        l1_load, wa_made = sem("l1_load"), sem("wa_made")
        x_turned, x_evac, seq_made, seq_saved = (sem(n) for n in ("x_turned", "x_evac", "seq_made", "seq_saved"))
        s1_turned, s1_saved, s1_store = sem("s1_turned"), sem("s1_saved"), sem("s1_store")
        g_part, g_turned, g_diag, g_all = sem("g_part"), sem("g_turned"), sem("g_diag"), sem("g_all")
        args_made, exps_made = sem("args_made"), sem("exps_made")
        c_s1 = [sem("c_s1_0"), sem("c_s1_1")]
        y_made, o_link = sem("y_made"), sem("o_link")
        o_load, h_turned, h_evac, z_made, z_neg, z_exp, z_used = (
            sem(n) for n in ("o_load", "h_turned", "h_evac", "z_made", "z_neg", "z_exp", "z_used"))
        fin, stored = sem("fin"), sem("stored")

        NCH = -(-T // CH)
        A_dve = Stage(sem("A_dve"), [f"hot{c}" for c in range(NCH)] + ["shift", "so", "idx", "prod", "red", "att",
                      "src", "attp", "diag", "eqs", "both", "any", "first", "keep", "code", "far", "mask", "back",
                      "gidc", "same", "prior", "one", "lead", "mul", "max", "wide", "put", "mrow", "rec", "gid", "end"])
        A_pe = Stage(sem("A_pe"), [f"list{c}" for c in range(NCH)] + ["turn", "qk", "rows", "lead"])
        A_act = Stage(sem("A_act"), ["xT0", "xT1", "k"])
        B_dve = Stage(sem("B_dve"), ["cur", "idx", "hot", "mx", "d", "cap", "S", "one", "rec",
                                     "add", "end"])
        B_pe = Stage(sem("B_pe"), ["sum"])
        B_act = Stage(sem("B_act"), ["exp"])
        C_dve = Stage(sem("C_dve"), ["cur", "curS", "idx", "hot", "sp", "g", "nb", "w", "wx"]
                      + [f"add{b}" for b in range(NB)] + ["end"])
        C_pe = Stage(sem("C_pe"), [f"corr{b}" for b in range(NB)])
        A_pool = Stage(sem("A_pool"), ["first"])
        O1_pool = Stage(sem("O1_pool"), ["first"])
        O2_pool = Stage(sem("O2_pool"), ["first"])
        O1_dve = Stage(sem("O1_dve"), ["cur", "cidx", "end"])
        O2_dve = Stage(sem("O2_dve"), ["cur", "cidx", "blank", "keep", "rec", "end"])
        owner_zero, owner_clear = sem("owner_zero"), sem("owner_clear")
        B_pool = Stage(sem("B_pool"), ["first"])
        C_pool = Stage(sem("C_pool"), ["first"])
        L_dve = Stage(sem("L_dve"), ["seqh", "Fh"] + [f"{k}{j}" for j in range(NB) for k in ("t1_", "t2_", "p_")]
                      + ["rd", "hid", "end"])
        L_pe = Stage(sem("L_pe"), [f"j{j}" for j in range(NB)])
        c_eb = sem("c_eb")
        kmade, k_link, ek_made = sem("kmade"), sem("k_link"), sem("ek_made")
        cnt_made, cnt_summed, bad_made, bad_summed, flag_made = (
            sem(n) for n in ("cnt_made", "cnt_summed", "bad_made", "bad_summed", "flag_made"))
        span_made, keys_spread, edge_link, edges_made = (
            sem(n) for n in ("span_made", "keys_spread", "edge_link", "edges_made"))
        tab_store, e_span, e_spread, e_arg, e_exp, e_hot, e_mul, e_agg, e_rec, e_hid, sc_made = (
            sem(n) for n in ("tab_store", "e_span", "e_spread", "e_arg", "e_exp", "e_hot", "e_mul",
                             "e_agg", "e_rec", "e_hid", "sc_made"))
        e_gather = [sem(f"e_gather{k}") for k in range(GR)]
        sp_half, sp_arg, pre_sc = sem("sp_half"), sem("sp_arg"), sem("pre_sc")
        e_link = sem("e_link")

        def tiles(eng, body, count):
            body(0)
            with eng.If(P < count):
                with eng.Fori(1, T) as u:
                    with eng.If(u * P < count):
                        body(u)

        def every_tile(eng, body, count):
            with eng.Fori(0, T) as u:
                with eng.If(u * P < count):
                    body(u)

        def misfits(eng):
            eng.wait_ge(flag_made, 1)
            return eng.value_load(badi[0:1, 0:1], min_val=0, max_val=4 * P)

        def how_many(eng):
            eng.wait_ge(nv_made, 1)
            return eng.value_load(nvali[0:1, 0:1], min_val=0, max_val=T * P)

        def bank(n, width=512):
            return ps[:, n, 0:width]

        RB = ps[:, 5:8, :].rearrange("p a b -> p (a b)")[:, 0:10 * P].rearrange("p (r e) -> p r e", r=10)
        NW = 2 * KT
        NG = NW + NB * KT

        def evac_count(g):
            return g // 2 + 1

        def group_out(g):
            if g < NW:
                return WT[:, g // KT, g % KT, :]
            b, q = divmod(g - NW, KT)
            return adjT[:, 4 * q:4 * q + 4, b * P:(b + 1) * P]

        def group_in(g):
            return bank(g % 4) if g < NW else bank(g % 4).rearrange("p (j i) -> p j i", j=4)

        seq = part(arenaA, 0, [NB, D])
        hid = seq
        x1 = ax
        Wseq = part(stage, 0, [KT, D])
        Wa = part(stage, 2048, [KT, 2, H1])
        xT = part(stage, 2304, [2, KT, P])
        wtmp = part(arenaA, 0, [KT, H1, D1])
        eT = part(arenaB, 0, [2, N])
        p_raw = part(arenaB, 0, [N])
        p_buf = part(arenaB, N, [2, N])
        seqh = part(arenaB, 3 * N, [NB, D1 + 1])
        eB = part(stage, 0, [2, N])
        ekb = sb("ekb", [P, NB, 18])
        erow = sb("erow", [P, NB * KE])
        eidx = sb("eidx", [P, NB * KE], I32)
        eend = sb("eend", [P, 2, NB])
        bad = sb("bad", [P, 4])
        badi = sb("badi", [P, 1], I32)
        key = part(arenaA, 4096, [N])
        ek = ekb[:]
        top = part(arenaA, 6144 + 288, [2, 64])
        scan = part(arenaA, 7680, [2, T])
        junk = part(arenaA, 7680 + 2 * T, [P])
        over = part(arenaA, 6144 + 416, [NB])
        kiota = iota[:, 0:16]
        pick = part(arenaB, 1536 + 2 * 4 * KE, [2, 4 * KE, 16])
        spot = part(arenaB, 2 * KE * P, [2, 4 * KE])
        span = part(arenaB, 0, [2, KE * P])
        spare = adjT[:].rearrange("p j i -> p (j i)").bitcast(F32)
        G = part(spare, 6144, [GR, KE, D + H1])
        ehot = part(stage, 0, [2, KE, P])
        espan = part(stage, 2 * KE * P, [2, KE * P])
        earg = part(stage, 4 * KE * P, [3, KE * H1])
        DEN = KE * 2 * H1
        sden = sb("sden", [P, 2, H1])
        sc = part(rec[:].rearrange("p t r -> p (t r)"), NB * 2 * H1, [NB, 2, H1])
        recw = rec[:].rearrange("p t r -> p (t r)")
        s12 = part(recw, 0, [NB, 2, H1])
        Fh = sb("Fh", [P, 2, NB])
        rden = sb("rden", [P, 2, 8])
        a12 = sb("a12", [P, 2, D1])
        gm = sb("gm", [P, 3, H1])
        M2 = sb("M2", [P, H1])
        EF = part(arenaB, 3 * N + NB * (D1 + 1), [4, NB, H1])
        z = part(recw, NB * 2 * H1, [2, NB, H1])
        Wo = part(spare, 0, [KT, D])
        hT = part(spare, 2048, [2, KT, P])
        zt = part(spare, 3072, [2, D])
        ze = part(spare, 4096, [2, D])
        zt2 = part(spare, 5120, [2, D])
        bo = bqk

        block = ctx.enter_context(nc.Block())

        @block.sync
        def _(sp):
            sp.wait_ge(cleared, 1)
            sp.dma_start(pr[:, 0:TC, :], pairs[0:TC * P, :].rearrange("(p t) c -> p t c", p=P)).then_inc(c_pr, 16)
            sp.dma_start(pr[0:TAIL, TC, :], pairs[TC * P:E, :]).then_inc(c_pr, 16)
            sp.dma_start(Wraw[:, 0], Wq.rearrange("(b p) d -> p b d", p=P)).then_inc(c_w, 16)
            sp.dma_start(Wraw[:, 1], Wk.rearrange("(b p) d -> p b d", p=P)).then_inc(c_w, 16)
            sp.dma_start(x_in, x.rearrange("(b p) d -> p b d", p=P)).then_inc(c_x, 16)
            sp.dma_start(bqk[:, 0, :], bq.rearrange("(o d) -> o d", o=1)).then_inc(c_b, 16)
            sp.dma_start(bqk[:, 1, :], bk.rearrange("(o d) -> o d", o=1)).then_inc(c_b, 16)
            for b in range(NB):
                if b >= 2:
                    sp.wait_ge(turned, NW + KT * (b - 1))
                    sp.wait_ge(row_summed, b - 1)
                    sp.wait_ge(row_diag, b - 1)
                sp.dma_start(arow[:, b % 2, :], adj[b * P:(b + 1) * P, :]).then_inc(c_row[b % 2], 16)
            sp.wait_ge(ax_made, NB)
            sp.dma_start(x_again, x.rearrange("(b p) d -> p b d", p=P)).then_inc(again, 16)
            sp.dma_start(a12[:, 0, :], a1.rearrange("(o d) -> o d", o=1).to_broadcast([P, D1])).then_inc(l1_load, 16)
            sp.dma_start(a12[:, 1, :], a2.rearrange("(o d) -> o d", o=1).to_broadcast([P, D1])).then_inc(l1_load, 16)
            sp.wait_ge(m_made, 1)
            count = how_many(sp)
            with sp.If(P < count):
                sp.wait_ge(owner_zero, 1)
                for b in range(NB):
                    sp.dma_start(owner.rearrange("(b p m) o -> b p (m o)", b=NB, p=P)[b], wide).then_inc(owner_clear, 16)
            sp.dma_start(mtab.rearrange("(b p) h -> p b h", p=P), mrow[:]).then_inc(m_store, 16)
            sp.dma_start(Wseq, W_seq.rearrange("(b p) d -> p b d", p=P)).then_inc(l1_load, 16)
            sp.dma_start(bo[:, 0, :], b_out.rearrange("(o d) -> o d", o=1)).then_inc(l1_load, 16)
            sp.wait_ge(w_made, 1)
            sp.dma_start(wtab.rearrange("(b p) h -> p b h", p=P), tab[:]).then_inc(w_store, 16)
            for b in range(NB):
                sp.wait_ge(seq_saved, 2 * (b + 1))
                sp.dma_start(seqtab[b * P:(b + 1) * P, 0:D], seq[:, b, :]).then_inc(tab_store, 16)
                sp.dma_start(seqtab[b * P:(b + 1) * P, D:D + H1], s12[:, b, 1, :]).then_inc(tab_store, 16)
            misfit = misfits(sp)
            with sp.If(misfit < 1):
                sp.dma_start(Wo, W_out.rearrange("(b p) d -> p b d", p=P)).then_inc(o_load, 16)
            with sp.If(0 < misfit):
                sp.wait_ge(s1_saved, 2)
                for k in range(2):
                    sp.dma_start(etab[k], eT[0:H1, k, :]).then_inc(s1_store, 16)
                sp.wait_ge(s1_store, 32)
                sp.wait_ge(seq_made, NB)
                sp.wait_ge(x_evac, NB)
                sp.dma_start(eB[:, 0, :], etab[0, 0:1, :].to_broadcast([P, N])).then_inc(c_eb, 16)
                sp.dma_start(eB[:, 1, :], etab[1, 0:1, :].to_broadcast([P, N])).then_inc(c_eb, 16)
                with sp.Fori(1, H1) as h:
                    sp.wait_ge(L_dve.sem, L_dve.after(h - 1, f"t2_{NB - 1}"))
                    sp.dma_start(eB[:, 0, :], etab[0, bass.ds(h, 1), :].to_broadcast([P, N])).then_inc(c_eb, 16)
                    sp.dma_start(eB[:, 1, :], etab[1, bass.ds(h, 1), :].to_broadcast([P, N])).then_inc(c_eb, 16)
                sp.wait_ge(L_dve.sem, L_dve.n * H1)
                sp.dma_start(Wo, W_out.rearrange("(b p) d -> p b d", p=P)).then_inc(o_load, 16)
            sp.wait_ge(tab_store, 32 * NB)
            for b in range(NB):
                sp.wait_ge(fin, b + 1)
                sp.dma_start(out[b * P:(b + 1) * P, :], x1[:, b, :]).then_inc(stored, 16)
            sp.wait_ge(stored, 16 * NB)

        @block.gpsimd
        def _(pool):
            g = nc.gpsimd
            g.memset(ident[:], 0.0).then_inc(masks, 1)
            g.memset(ones[:], 1.0).then_inc(masks, 1)
            g.memset(bias[:, 0:1], SELF).then_inc(masks, 1)
            g.memset(bias[:, 1:2], EPS).then_inc(masks, 1)
            g.iota(iota[:], [[1, N]], base=0, channel_multiplier=0).then_inc(masks, 1)
            g.iota(rowid[:], [[P, NB]], base=0, channel_multiplier=1,
                   allow_small_or_imprecise_dtypes=True).then_inc(masks, 1)
            g.iota(gid[:], [[1, 1]], base=0, channel_multiplier=1,
                   allow_small_or_imprecise_dtypes=True).then_inc(masks, 1)
            pool.wait_ge(masks, 7)
            g.affine_select(out=ident[:], in_=ident[:], compare_op=ALU.not_equal, fill=1.0, base=0,
                            pattern=[[-1, P]], channel_multiplier=1).then_inc(masks, 1)
            g.affine_select(out=before[:], in_=ones[:], compare_op=ALU.is_gt, fill=0.0, base=0,
                            pattern=[[-1, P]], channel_multiplier=1).then_inc(masks, 1)
            g.affine_select(out=below[:], in_=ones[:], compare_op=ALU.is_gt, fill=0.0, base=0,
                            pattern=[[1, P]], channel_multiplier=-1).then_inc(masks, 1)
            pool.wait_ge(idx_made, 1)
            for t in range(T):
                g.indirect_dma_start(out=avals[:, t:t + 1], out_offset=None, in_=adj_flat,
                                     in_offset=bass.IndirectOffsetOnAxis(ap=aidx[:, t:t + 1], axis=0)
                                     ).then_inc(c_av, 16)
            count = None

            def pass_gate(k, stage, step):
                g.tensor_tensor(gate[:, k:k + 1], ones[:, 0:1], ones[:, 1:2], ALU.mult).then_inc(stage.sem, 1)

            def loop_a(u):
                pool.wait_ge(A_dve.sem, A_dve.after(u, "idx"))
                pass_gate(0, A_pool, "first")
                for w, src in ((0, x), (1, x)):
                    g.indirect_dma_start(out=xso[:, w, :], out_offset=None, in_=src,
                                         in_offset=bass.IndirectOffsetOnAxis(ap=curi[:, w:w + 1], axis=0)
                                         ).then_inc(a_gather, 16)

            def loop_put(u):
                pool.wait_ge(O1_dve.sem, O1_dve.after(u, "cidx"))
                pass_gate(1, O1_pool, "first")
                g.indirect_dma_start(out=owner, out_offset=bass.IndirectOffsetOnAxis(ap=cidx[:, 0:1], axis=0),
                                     in_=cur[:, 11:12], in_offset=None, bounds_check=N * N - 1,
                                     oob_is_err=False).then_inc(a_scatter, 16)

            def loop_get(u):
                pool.wait_ge(O2_dve.sem, O2_dve.after(u, "blank"))
                pass_gate(2, O2_pool, "first")
                g.indirect_dma_start(out=winner[:], out_offset=None, in_=owner,
                                     in_offset=bass.IndirectOffsetOnAxis(ap=cidx[:, 0:1], axis=0),
                                     bounds_check=N * N - 1, oob_is_err=False).then_inc(b_own, 16)

            def loop_b(u):
                pool.wait_ge(B_dve.sem, B_dve.after(u, "idx"))
                pass_gate(2, B_pool, "first")
                g.indirect_dma_start(out=mg[:], out_offset=None, in_=mtab,
                                     in_offset=bass.IndirectOffsetOnAxis(ap=curi[:, 0:1], axis=0)).then_inc(b_m, 16)

            def loop_c(u):
                pool.wait_ge(C_dve.sem, C_dve.after(u, "idx"))
                pass_gate(3, C_pool, "first")
                g.indirect_dma_start(out=xso[:, 1, :], out_offset=None, in_=x,
                                     in_offset=bass.IndirectOffsetOnAxis(ap=curi[:, 1:2], axis=0)
                                     ).then_inc(c_gather, 16)
                g.indirect_dma_start(out=tg[:], out_offset=None, in_=wtab,
                                     in_offset=bass.IndirectOffsetOnAxis(ap=curi[:, 0:1], axis=0)
                                     ).then_inc(c_gather, 16)

            count = how_many(pool)
            tiles(pool, loop_a, count)
            with pool.If(P < count):
                pool.wait_ge(owner_clear, 16 * NB)
                every_tile(pool, loop_put, count)
                every_tile(pool, loop_get, count)
            pool.wait_ge(m_store, 16)
            tiles(pool, loop_b, count)
            pool.wait_ge(w_store, 16)
            tiles(pool, loop_c, count)
            misfit = misfits(pool)
            with pool.If(misfit < 1):
                pool.wait_ge(edges_made, NB // 4)
                pool.wait_ge(tab_store, 32 * NB)
                for b in range(NB):
                    if b >= GR:
                        pool.wait_ge(e_agg, b - GR + 1)
                    for k in range(KE):
                        g.indirect_dma_start(out=G[:, b % GR, k, :], out_offset=None, in_=seqtab,
                                             in_offset=bass.IndirectOffsetOnAxis(
                                                 ap=eidx[:, b * KE + k:b * KE + k + 1], axis=0)
                                             ).then_inc(e_gather[b % GR], 16)


        @block.tensor
        def _(pe):
            t = nc.tensor
            pe.wait_ge(masks, 10)

            def turn_group(g):
                if g >= 4:
                    pe.wait_ge(evac_a if g % 2 else evac_d, evac_count(g - 4))
                for n in range(4):
                    if g < NW:
                        src = Wraw[:, g // KT, n, (g % KT) * P:(g % KT + 1) * P]
                    else:
                        b, q = divmod(g - NW, KT)
                        src = arow[:, b % 2, (4 * q + n) * P:(4 * q + n + 1) * P]
                    ins = t.transpose(bank(g % 4)[:, n * P:(n + 1) * P], src, ident[:])
                ins.then_inc(turned, 1)

            def multiply(b):
                last = NW + KT * b + KT - 1
                pe.wait_ge(evac_a, evac_count(last))
                pe.wait_ge(evac_d, evac_count(last - 1))
                if b >= 2:
                    pe.wait_ge(ax_saved, b - 1)
                for j in range(NB):
                    for w in range(2):
                        ins = t.matmul(bank(4 + b % 2), adjT[:, j, b * P:(b + 1) * P], xsplit[:, w, j, :],
                                       start=(j == 0 and w == 0), stop=(j == NB - 1 and w == 1))
                ins.then_inc(ax_made, 1)

            pe.wait_ge(c_w, 32)
            pe.wait_ge(low_done, NB)
            for g in range(NW):
                turn_group(g)
            for b in range(NB + 1):
                if b < NB:
                    pe.wait_ge(c_row[b % 2], 16 * (b // 2 + 1))
                    for q in range(KT):
                        turn_group(NW + KT * b + q)
                if b >= 1:
                    multiply(b - 1)

            pe.wait_ge(cnt_made, 1)
            t.matmul(ps[:, 6, 0:NB], below[:], mv[:, :, 0], start=True, stop=True)
            t.matmul(ps[:, 6, NB:2 * NB], ones[:], mv[:, :, 0], start=True, stop=True).then_inc(cnt_summed, 1)
            pe.wait_ge(bad_made, 1)
            t.matmul(ps[:, 6, 64:65], ones[:], bad[:, 3:4], start=True, stop=True).then_inc(bad_summed, 1)
            pe.wait_ge(tot_made, 1)
            t.matmul(ps[:, 6, 0:1], below[:], nval[:, 0:1], start=True, stop=True)
            t.matmul(ps[:, 6, 1:2], ones[:], nval[:, 0:1], start=True, stop=True).then_inc(off_made, 1)

            def loop_a(u):
                D_, M_, S_ = A_dve, A_pe, A_act
                for c in range(NCH):
                    pe.wait_ge(D_.sem, D_.after(u, f"hot{c}"))
                    for tt in range(c * CH, min(T, (c + 1) * CH)):
                        ins = t.matmul(ps[:, 0, 0:2], ohot[:, c % 2, tt - c * CH, :], prh[:, tt, :],
                                       start=(tt == 0), stop=(tt == T - 1))
                    ins.then_inc(M_.sem, 1)
                pe.wait_ge(a_gather, 32 * (u + 1))
                for w in range(2):
                    for k in range(KT):
                        ins = t.transpose(ps[:, 1 + w, k * P:(k + 1) * P], xso[:, w, k * P:(k + 1) * P], ident[:])
                ins.then_inc(M_.sem, 1)
                pe.wait_ge(S_.sem, S_.after(u, "xT1"))
                for w in range(2):
                    for k in range(KT):
                        t.matmul(bank(3 + w), xsoT[:, w, k, :], WT[:, w, k, :], start=(k == 0), stop=False)
                    ins = t.matmul(bank(3 + w), ones[0:1, :], bqk[0:1, w, :], start=False, stop=True)
                ins.then_inc(M_.sem, 1)
                pe.wait_ge(D_.sem, D_.after(u, "diag"))
                flat = diag.rearrange("p r e -> p (r e)")
                for k in range(0, 10 * P, 512):
                    n = min(512, 10 * P - k)
                    ins = t.matmul(ps[:, 5 + k // 512, 0:n], ones[:], flat[:, k:k + n], start=True, stop=True)
                ins.then_inc(M_.sem, 1)
                pe.wait_ge(D_.sem, D_.after(u, "put"))
                for b in range(NB):
                    ins = t.matmul(ps[:, 1, b * H0:(b + 1) * H0], wide[:, b * P:(b + 1) * P], attv[:, 1, :],
                                   start=True, stop=True)
                ins.then_inc(M_.sem, 1)

            def loop_b(u):
                pe.wait_ge(B_dve.sem, B_dve.after(u, "rec"))
                for b in range(NB):
                    ins = t.matmul(ps[:, 0, b * 9:(b + 1) * 9], wide[:, b * P:(b + 1) * P], curS[:],
                                   start=True, stop=True)
                ins.then_inc(B_pe.sem, 1)

            def loop_c(u):
                pe.wait_ge(C_dve.sem, C_dve.after(u, "wx"))
                for b in range(NB):
                    if b >= 8:
                        pe.wait_ge(C_dve.sem, C_dve.after(u, f"add{b - 8}"))
                    t.matmul(bank(b % 8), wide[:, b * P:(b + 1) * P], xso[:, 0, :],
                             start=True, stop=True).then_inc(C_pe.sem, 1)

            count = how_many(pe)
            pe.wait_ge(c_b, 32)
            tiles(pe, loop_a, count)
            tiles(pe, loop_b, count)
            tiles(pe, loop_c, count)

            def spread_keys(b):
                pe.wait_ge(span_made, b + 1)
                if b % 4 == 0 and b >= 8:
                    pe.wait_ge(edges_made, b // 4 - 1)
                for k in range(KE):
                    o_ = (b % 4 * KE + k) * 18
                    ins = t.matmul(ps[:, 6 + b // 4 % 2, o_:o_ + 18], span[:, b % 2, k * P:(k + 1) * P], ek[:, b, :],
                                   start=True, stop=True)
                ins.then_inc(keys_spread, 1)

            pe.wait_ge(wa_made, 2)
            for b in range(NB):
                pe.wait_ge(x1_made, b + 1)
                if b >= 2:
                    pe.wait_ge(x_evac, b - 1)
                for k in range(KT):
                    ins = t.transpose(bank(b % 2)[:, k * P:(k + 1) * P], x1[:, b, k * P:(k + 1) * P], ident[:])
                ins.then_inc(x_turned, 1)
                pe.wait_ge(x_evac, b + 1)
                if b >= 2:
                    pe.wait_ge(seq_saved, 2 * (b - 1))
                for k in range(KT):
                    t.matmul(bank(2 + b % 2), xT[:, b % 2, k, :], Wseq[:, k, :], start=(k == 0), stop=(k == KT - 1))
                for k in range(KT):
                    ins = t.matmul(ps[:, 4 + b % 2, 0:2 * H1], xT[:, b % 2, k, :],
                                   Wa[:, k].rearrange("p s h -> p (s h)"), start=(k == 0), stop=(k == KT - 1))
                ins.then_inc(seq_made, 1)
                if b >= 1:
                    spread_keys(b - 1)
            spread_keys(NB - 1)
            pe.wait_ge(edges_made, NB // 4)
            pe.wait_ge(g_part, 1)
            t.transpose(ps[0:H1, 6, 0:P], gm[:, 0, :], ident[:]).then_inc(g_turned, 1)
            pe.wait_ge(g_diag, 1)
            t.matmul(ps[:, 7, 0:H1], ones[0:H1, :], gm[0:H1, 1, :], start=True, stop=True).then_inc(g_all, 1)
            def spread(b):
                pe.wait_ge(e_span, b + 1)
                if b >= 2:
                    pe.wait_ge(e_rec, b - 1)
                for k in range(KE):
                    ins = t.matmul(ps[:, b % 2, k * 2 * H1:(k + 1) * 2 * H1], espan[:, b % 2, k * P:(k + 1) * P],
                                   sc[:, b].rearrange("p s h -> p (s h)"), start=True, stop=True)
                ins.then_inc(e_spread, 1)

            def turn_hidden(b):
                if b >= 2:
                    pe.wait_ge(h_evac, b - 1)
                for k in range(KT):
                    ins = t.transpose(bank(4 + b % 2)[:, k * P:(k + 1) * P], hid[:, b, k * P:(k + 1) * P], ident[:])
                ins.then_inc(h_turned, 1)

            def project(b):
                if b == 0:
                    pe.wait_ge(o_load, 16)
                pe.wait_ge(h_evac, b + 1)
                if b >= 2:
                    pe.wait_ge(z_used, b - 1)
                    pe.wait_ge(z_neg, b - 1)
                for k in range(KT):
                    t.matmul(bank(6 + b % 2), hT[:, b % 2, k, :], Wo[:, k, :], start=(k == 0), stop=False)
                t.matmul(bank(6 + b % 2), ones[0:1, :], bo[0:1, 0, :], start=False, stop=True).then_inc(z_made, 1)

            def pe_dense():
                pe.wait_ge(exps_made, 2)
                for k in range(2):
                    if k:
                        pe.wait_ge(s1_saved, 1)
                    for b in range(NB):
                        ins = t.transpose(ps[0:H1, b // 4, (b % 4) * P:(b % 4 + 1) * P], EF[:, k, b, :], ident[:])
                    ins.then_inc(s1_turned, 1)

                pe.wait_ge(s1_saved, 2)
                with pe.Fori(0, H1) as h:
                    for j in range(NB):
                        pe.wait_ge(L_dve.sem, L_dve.after(h, f"p_{j}"))
                        for b in range(NB):
                            ins = t.matmul(ps[:, b // 8, (b % 8) * (D1 + 1):(b % 8 + 1) * (D1 + 1)],
                                           p_buf[:, j % 2, b * P:(b + 1) * P], seqh[:, j, :],
                                           start=(j == 0 and b % 8 == 0), stop=(j == NB - 1), skip_group_check=True)
                        ins.then_inc(L_pe.sem, 1)


            misfit = misfits(pe)
            with pe.If(misfit < 1):
                pe.wait_ge(sc_made, 1)
                spread(0)
                for b in range(NB):
                    if b + 1 < NB:
                        spread(b + 1)
                    if b >= 2:
                        pe.wait_ge(e_hid, b - 1)
                        turn_hidden(b - 2)
                    if b >= 3:
                        project(b - 3)
                    for k in range(KE):
                        pe.wait_ge(e_mul, b * KE + k + 1)
                        t.matmul(bank(2 + b % 2), ehot[:, b % 2, k, :], G[:, b % GR, k, 0:D],
                                 start=(k == 0), stop=(k == KE - 1))
                        ins = t.matmul(ps[:, b % 2, DEN:DEN + H1], ehot[:, b % 2, k, :], G[:, b % GR, k, D:D + H1],
                                       start=(k == 0), stop=(k == KE - 1), skip_group_check=True)
                    ins.then_inc(e_agg, 1)
                project(NB - 3)
                for b in range(NB - 2, NB):
                    pe.wait_ge(e_hid, b + 1)
                    turn_hidden(b)
                    project(b)
            with pe.If(0 < misfit):
                pe_dense()
                pe.wait_ge(L_dve.sem, L_dve.n * H1)
                for b in range(NB):
                    turn_hidden(b)
                    project(b)

        @block.scalar
        def _(act):
            s = nc.scalar
            act.wait_ge(c_x, 16)
            for b in range(NB):
                s.copy(xsplit[:, 0, b, :], x_in[:, b, :]).then_inc(high_done, 1)
            for g in range(1, NG, 2):
                act.wait_ge(turned, g + 1)
                s.copy(group_out(g), group_in(g)).then_inc(evac_a, 1)
                if g >= NW and (g - NW) % KT == 1:
                    b = (g - NW) // KT
                    if b >= 1:
                        act.wait_ge(row_summed, b)
                    s.activation(ohot[:].rearrange("p a b c -> p (a b c)")[:, 0:N], arow[:, b % 2, :], ACT.Identity,
                                 accum_out=deg[:, 0, b:b + 1]).then_inc(row_summed, 1)

            def loop_a(u):
                act.wait_ge(A_pe.sem, A_pe.after(u, "turn"))
                for w in range(2):
                    s.copy(xsoT[:, w].rearrange("p k e -> p (k e)"), bank(1 + w)).then_inc(A_act.sem, 1)
                act.wait_ge(A_pe.sem, A_pe.after(u, "qk"))
                s.copy(ksb, bank(4)).then_inc(A_act.sem, 1)

            def loop_b(u):
                act.wait_ge(B_dve.sem, B_dve.after(u, "cap"))
                s.activation(attv[:, 1, :], attv[:, 0, :], ACT.Exp).then_inc(B_act.sem, 1)

            count = how_many(act)
            tiles(act, loop_a, count)
            tiles(act, loop_b, count)
            act.wait_ge(mx_made, 1)
            s.activation(rt[:, 1], rt[:, 0], ACT.Exp, scale=-1.0).then_inc(e_made, 1)
            s.activation(rt[:, 2], rt[:, 0], ACT.Exp, scale=-1.0, bias=bias[:, 0:1]).then_inc(e_made, 1)
            act.wait_ge(again, 16)
            act.wait_ge(sw_made, 1)
            for b in range(NB):
                s.activation(x_again[:, b, :], x_again[:, b, :], ACT.Identity,
                             scale=selfw[:, 1, b:b + 1]).then_inc(scaled, 1)
            act.wait_ge(var_made, NB)
            s.activation(rstd[:, 0, :], mv[:, :, 1], ACT.Sqrt, bias=bias[:, 1:2]).then_inc(root_made, 1)
            for b in range(NB):
                act.wait_ge(x_turned, b + 1)
                if b >= 2:
                    act.wait_ge(seq_made, b - 1)
                s.copy(xT[:, b % 2].rearrange("p k e -> p (k e)"), bank(b % 2)).then_inc(x_evac, 1)
            def copy_turned(b):
                act.wait_ge(h_turned, b + 1)
                if b >= 2:
                    act.wait_ge(z_made, b - 1)
                s.copy(hT[:, b % 2].rearrange("p k e -> p (k e)"), bank(4 + b % 2)).then_inc(h_evac, 1)

            def elu_part(b):
                act.wait_ge(z_made, b + 1)
                if b >= 2:
                    act.wait_ge(z_used, b - 1)
                s.activation(zt[:, b % 2, :], bank(6 + b % 2), ACT.Relu, scale=-1.0).then_inc(z_neg, 1)
                act.wait_ge(z_neg, b + 1)
                s.activation(ze[:, b % 2, :], zt[:, b % 2, :], ACT.Exp, scale=-1.0).then_inc(z_exp, 1)

            misfit = misfits(act)
            with act.If(misfit < 1):
                for b in range(NB):
                    act.wait_ge(e_arg, b + 1)
                    s.activation(G[:, b % GR, :, D:D + H1], earg[:, 2].rearrange("p (k h) -> p k h", k=KE),
                                 ACT.Exp).then_inc(e_exp, 1)
                    if b >= 2:
                        copy_turned(b - 2)
                    if b >= 4:
                        elu_part(b - 4)
                for b in range(NB - 4, NB - 2):
                    elu_part(b)
                for b in range(NB - 2, NB):
                    copy_turned(b)
                    elu_part(b)
            with act.If(0 < misfit):
                act.wait_ge(args_made, 1)
                for k in range(2):
                    s.activation(EF[:, k], z[:, k], ACT.Exp).then_inc(exps_made, 1)
                act.wait_ge(args_made, 2)
                s.activation(EF[:, 2], z[:, 0], ACT.Exp).then_inc(exps_made, 1)
                s.activation(EF[:, 3], z[:, 0], ACT.Exp, scale=SLOPE).then_inc(exps_made, 1)
                for k in range(2):
                    act.wait_ge(s1_turned, k + 1)
                    s.copy(eT[0:H1, k, :], ps[0:H1, 0:4, :].rearrange("p a b -> p (a b)")).then_inc(s1_saved, 1)
                for b in range(NB):
                    copy_turned(b)
                    elu_part(b)
            act.wait_ge(var_made, 2 * NB)
            s.activation(rstd[:, 0, :], mv[:, :, 1], ACT.Sqrt, bias=bias[:, 1:2]).then_inc(root_made, 1)

        @block.vector
        def _(dve):
            v = nc.vector
            links = [0]

            def link(ins):
                links[0] += 1
                ins.then_inc(link_d, 1)
                dve.wait_ge(link_d, links[0])

            v.memset(racc[:], 0.0)
            v.memset(mrow[:], 0.0)
            v.memset(winner[:], -1.0)
            v.memset(cur[:], 0.0)
            v.memset(pr[:], 0).then_inc(cleared, 1)
            dve.wait_ge(c_pr, 32)
            link(v.tensor_copy(prf[:], pr[:]))
            link(v.tensor_scalar_add(prh[:], prf[:], 1.0))
            v.scalar_tensor_tensor(aidx[:], prf[:, :, 0], float(N), prf[:, :, 1], ALU.mult, ALU.add).then_inc(idx_made, 1)
            for b in range(NB):
                dve.wait_ge(high_done, b + 1)
                v.tensor_tensor(xsplit[:, 1, b, :], x_in[:, b, :], xsplit[:, 0, b, :], ALU.subtract).then_inc(low_done, 1)

            def save_ax(b):
                dve.wait_ge(ax_made, b + 1)
                v.tensor_copy(ax[:, b, :], bank(4 + b % 2)).then_inc(ax_saved, 1)

            def find_neighbours(b):
                def chain(ins):
                    kl[0] += 1
                    ins.then_inc(k_link, 1)
                    dve.wait_ge(k_link, kl[0])

                seg = N // 8
                chain(v.scalar_tensor_tensor(key, iota[:], 1.0, arow[:, b % 2, :], ALU.add, ALU.mult))
                for k in range(8):
                    ins = v.max(top[:, 0, 8 * k:8 * k + 8], key[:, k * seg:(k + 1) * seg])
                chain(ins)
                v.tensor_reduce(over[:, b:b + 1], top[:, 0].rearrange("p (s k) -> p s k", k=8)[:, :, 7], X, ALU.max)
                chain(v.max(ek[:, b, 0:8], top[:, 0]))
                chain(v.match_replace(top[:, 1], ek[:, b, 0:8], top[:, 0], 0.0))
                chain(v.max(ek[:, b, 8:16], top[:, 1]))

            def measure():
                def chain(ins):
                    kl[0] += 1
                    ins.then_inc(k_link, 1)
                    dve.wait_ge(k_link, kl[0])

                dve.wait_ge(row_summed, NB)
                chain(v.tensor_scalar_add(ek[:, :, 17], rowid[:, 0:1].to_broadcast([P, NB]), 1.0))
                v.tensor_copy(mv[:, :, 0], deg[:, 0, :]).then_inc(cnt_made, 1)
                dve.wait_ge(cnt_summed, 1)
                v.tensor_copy(ek[:, :, 16], ps[:, 6, 0:NB])
                v.tensor_copy(eend[:, 0, :], ps[:, 6, 0:NB])
                v.tensor_reduce(bad[:, 0:1], over, X, ALU.max)
                v.tensor_reduce(bad[:, 1:2], deg[:, 0, :], X, ALU.max)
                chain(v.tensor_reduce(bad[:, 2:3], ps[:, 6, NB:2 * NB], X, ALU.max))
                v.tensor_tensor(eend[:, 1, :], eend[:, 0, :], deg[:, 0, :], ALU.add)
                v.tensor_scalar(bad[:, 0:1], bad[:, 0:1], 0.0, None, ALU.is_gt)
                v.tensor_scalar(bad[:, 1:2], bad[:, 1:2], 16.0, None, ALU.is_gt)
                chain(v.tensor_scalar(bad[:, 2:3], bad[:, 2:3], float(KE * P), None, ALU.is_gt))
                v.tensor_reduce(bad[:, 3:4], bad[:, 0:3], X, ALU.add).then_inc(bad_made, 1)
                dve.wait_ge(bad_summed, 1)
                v.tensor_copy(badi[:], ps[:, 6, 64:65]).then_inc(flag_made, 1)

            def list_edges(b):
                def chain(ins):
                    kl[0] += 1
                    ins.then_inc(k_link, 1)
                    dve.wait_ge(k_link, kl[0])

                if True:
                    if b >= 2:
                        dve.wait_ge(keys_spread, b - 1)
                    chain(v.tensor_scalar(span[:, b % 2], iota[:, 0:KE * P], eend[:, 1, b:b + 1], None, ALU.is_lt))
                    v.scalar_tensor_tensor(span[:, b % 2], iota[:, 0:KE * P], eend[:, 0, b:b + 1], span[:, b % 2],
                                           ALU.is_ge, ALU.mult).then_inc(span_made, 1)
                    dve.wait_ge(span_made, b + 1)
                    if b % 4 < 3:
                        return
                    c = b // 4
                    dve.wait_ge(keys_spread, b + 1)
                    sp_ = ps[:, 6 + c % 2, 0:4 * KE * 18].rearrange("p (a k) -> p a k", k=18)
                    chain(v.tensor_copy(pick[:, 1], sp_[:, :, 0:16]))
                    for q in range(4):
                        ins = v.tensor_tensor(spot[:, 0, q * KE:(q + 1) * KE], rowid[:, 0:KE],
                                              sp_[:, q * KE:(q + 1) * KE, 16], ALU.subtract)
                    chain(ins)
                    chain(v.tensor_tensor(pick[:, 0], kiota.unsqueeze(1).to_broadcast([P, 4 * KE, 16]),
                                          spot[:, 0].unsqueeze(2).to_broadcast([P, 4 * KE, 16]), ALU.is_equal))
                    chain(v.tensor_tensor(pick[:, 0], pick[:, 0], pick[:, 1], ALU.mult))
                    chain(v.tensor_reduce(spot[:, 1], pick[:, 0], X, ALU.add))
                    chain(v.tensor_scalar(eidx[:, c * 4 * KE:(c + 1) * 4 * KE], spot[:, 1], -1.0, 0.0, ALU.add, ALU.max))
                    chain(v.tensor_scalar_add(erow[:, c * 4 * KE:(c + 1) * 4 * KE], sp_[:, :, 17], -1.0))
                    v.memset(wv[:, 3:4], 0.0).then_inc(edges_made, 1)
                    dve.wait_ge(edges_made, c + 1)

            kl = [0]
            dve.wait_ge(masks, 10)
            for g in range(0, NG, 2):
                dve.wait_ge(turned, g + 1)
                v.tensor_copy(group_out(g), group_in(g)).then_inc(evac_d, 1)
                if g >= NW and (g - NW) % KT == 2:
                    b = (g - NW) // KT
                    find_neighbours(b)
                    if b >= 1:
                        dve.wait_ge(row_diag, b)
                    v.tensor_tensor_reduce(junk, arow[:, b % 2, b * P:(b + 1) * P], ident[:], 1.0, 0.0,
                                           ALU.mult, ALU.add, deg[:, 1, b:b + 1]).then_inc(row_diag, 1)
                    if b >= 1:
                        save_ax(b - 1)
            save_ax(NB - 1)
            measure()

            dve.wait_ge(c_av, 16 * T)
            link(v.tensor_tensor(scan[:, 0, :], prf[:, :, 0], prf[:, :, 1], ALU.not_equal))
            link(v.tensor_tensor(avals[:], avals[:], scan[:, 0, :], ALU.mult))
            link(v.tensor_copy(scan[:, 0, :], avals[:]))
            side, d = 0, 1
            while d < T:
                v.tensor_copy(scan[:, 1 - side, 0:d], scan[:, side, 0:d])
                link(v.tensor_tensor(scan[:, 1 - side, d:T], scan[:, side, d:T], scan[:, side, 0:T - d], ALU.add))
                side, d = 1 - side, 2 * d
            v.tensor_copy(nval[:, 0:1], scan[:, side, T - 1:T]).then_inc(tot_made, 1)
            dve.wait_ge(off_made, 1)
            link(v.tensor_copy(nval[:, 1:2], ps[:, 6, 0:1]))
            v.tensor_copy(nvali[:], ps[:, 6, 1:2]).then_inc(nv_made, 1)
            link(v.scalar_tensor_tensor(pos[:], scan[:, side, :], nval[:, 1:2], avals[:], ALU.add, ALU.mult))
            link(v.tensor_scalar_add(pos[:], pos[:], -1.0))

            def at(rows, u):
                return rows[:, u, :] if isinstance(u, int) else rows[:, bass.ds(u, 1), :]

            def as_slot(tile, u):
                return tile[:] if isinstance(u, int) else tile[:].unsqueeze(1)

            def loop_a(u):
                S = A_dve

                def own(step):
                    dve.wait_ge(S.sem, S.after(u, step))

                for c in range(NCH):
                    n = min(CH, T - c * CH)
                    if c >= 2:
                        dve.wait_ge(A_pe.sem, A_pe.after(u, f"list{c - 2}"))
                    v.tensor_tensor(ohot[:, c % 2, 0:n, :], pos[:, c * CH:c * CH + n].unsqueeze(2).to_broadcast([P, n, P]),
                                    iota[:, 0:P].unsqueeze(1).to_broadcast([P, n, P]), ALU.is_equal).then_inc(S.sem, 1)
                own(f"hot{NCH - 1}")
                v.tensor_scalar_add(pos[:], pos[:], -float(P)).then_inc(S.sem, 1)
                dve.wait_ge(A_pe.sem, A_pe.after(u, f"list{NCH - 1}"))
                v.tensor_scalar_add(cur[:, 0:2], ps[:, 0, 0:2], -1.0).then_inc(S.sem, 1)
                own("so")
                v.tensor_scalar_max(curi[:], cur[:, 0:2], 0.0).then_inc(S.sem, 1)
                dve.wait_ge(A_act.sem, A_act.after(u, "k"))
                v.tensor_tensor(prod, bank(3), ksb, ALU.mult).then_inc(S.sem, 1)
                own("prod")
                v.tensor_reduce(attv[:, 0, :], prod.rearrange("p (h d) -> p h d", h=H0), X, ALU.add).then_inc(S.sem, 1)
                own("red")
                v.tensor_scalar_mul(cur[:, 2:2 + H0], attv[:, 0, :], float(D0) ** -0.5).then_inc(S.sem, 1)
                own("att")
                v.tensor_copy(rowsrc[:, 0:2], cur[:, 0:2]).then_inc(S.sem, 1)
                v.tensor_scalar_max(rowsrc[:, 2:10], cur[:, 2:10], 0.0).then_inc(S.sem, 1)
                own("attp")
                v.tensor_tensor(diag, ident[:].unsqueeze(1).to_broadcast([P, 10, P]),
                                rowsrc[:].unsqueeze(2).to_broadcast([P, 10, P]), ALU.mult).then_inc(S.sem, 1)
                dve.wait_ge(A_pe.sem, A_pe.after(u, "rows"))
                e1, e2 = part(stage, 1024, [P]), part(stage, 1024 + P, [P])
                v.scalar_tensor_tensor(e1, RB[:, 0, :], cur[:, 0:1], before[:], ALU.is_equal, ALU.mult).then_inc(S.sem, 1)
                own("eqs")
                v.scalar_tensor_tensor(e2, RB[:, 1, :], cur[:, 1:2], e1, ALU.is_equal, ALU.mult).then_inc(S.sem, 1)
                own("both")
                v.tensor_reduce(tmp[:, 0:1], e2, X, ALU.max).then_inc(S.sem, 1)
                own("any")
                v.tensor_scalar(tmp[:, 1:2], tmp[:, 0:1], -1.0, 1.0, ALU.mult, ALU.add).then_inc(S.sem, 1)
                own("first")
                v.scalar_tensor_tensor(cur[:, 10:11], cur[:, 0:1], 0.0, tmp[:, 1:2], ALU.is_ge, ALU.mult).then_inc(S.sem, 1)
                own("keep")
                v.scalar_tensor_tensor(tmp[:, 2:3], cur[:, 0:1], float(N), cur[:, 1:2], ALU.mult, ALU.add).then_inc(S.sem, 1)
                own("code")
                v.tensor_scalar_add(tmp[:, 3:4], tmp[:, 2:3], -FAR).then_inc(S.sem, 1)
                own("far")
                v.tensor_tensor(tmp[:, 4:5], tmp[:, 3:4], cur[:, 10:11], ALU.mult).then_inc(S.sem, 1)
                own("mask")
                v.tensor_scalar_add(cur[:, 12:13], tmp[:, 4:5], FAR).then_inc(S.sem, 1)
                own("back")
                v.tensor_copy(cur[:, 11:12], gid[:]).then_inc(S.sem, 1)
                same, prior = part(stage, 1024 + 2 * P, [P]), part(stage, 1024 + 3 * P, [P])
                v.tensor_scalar(same, RB[:, 0, :], cur[:, 0:1], None, ALU.is_equal).then_inc(S.sem, 1)
                own("same")
                v.tensor_tensor(prior, same, before[:], ALU.mult).then_inc(S.sem, 1)
                own("prior")
                v.tensor_reduce(tmp[:, 5:6], prior, X, ALU.max).then_inc(S.sem, 1)
                own("one")
                v.tensor_scalar(tmp[:, 6:7], tmp[:, 5:6], -1.0, 1.0, ALU.mult, ALU.add).then_inc(S.sem, 1)
                v.tensor_tensor(prod8, RB[:, 2:10, :], same.unsqueeze(1).to_broadcast([P, H0, P]),
                                ALU.mult).then_inc(S.sem, 1)
                own("mul")
                v.tensor_reduce(mg[:], prod8, X, ALU.max).then_inc(S.sem, 1)
                v.tensor_scalar(wide, iota[:], cur[:, 0:1], None, ALU.is_equal).then_inc(S.sem, 1)
                own("max")
                v.tensor_scalar(attv[:, 1, :], mg[:], tmp[:, 6:7], None, ALU.mult).then_inc(S.sem, 1)
                dve.wait_ge(A_pe.sem, A_pe.after(u, "lead"))
                v.tensor_tensor(mrow[:], mrow[:], ps[:, 1, 0:NB * H0].rearrange("p (b h) -> p b h", b=NB),
                                ALU.max).then_inc(S.sem, 1)
                v.tensor_scalar_mul(at(rec, u), as_slot(cur, u), 1.0).then_inc(S.sem, 1)
                own("rec")
                v.tensor_scalar_add(gid[:], gid[:], float(P)).then_inc(S.sem, 1)
                own("gid")
                dve.wait_ge(A_pool.sem, A_pool.after(u, "first"))
                v.memset(wv[:, 3:4], 0.0).then_inc(S.sem, 1)

            def loop_put(u):
                S = O1_dve
                v.tensor_scalar_mul(cur[:].unsqueeze(1), rec[:, bass.ds(u, 1), :], 1.0).then_inc(S.sem, 1)
                dve.wait_ge(S.sem, S.after(u, "cur"))
                v.tensor_copy(cidx[:], cur[:, 12:13]).then_inc(S.sem, 1)
                dve.wait_ge(a_scatter, 16 * (u + 1))
                dve.wait_ge(O1_pool.sem, O1_pool.after(u, "first"))
                dve.wait_ge(S.sem, S.after(u, "cidx"))
                v.memset(wv[:, 3:4], 0.0).then_inc(S.sem, 1)

            def loop_get(u):
                S = O2_dve

                def own(step):
                    dve.wait_ge(S.sem, S.after(u, step))

                v.tensor_scalar_mul(cur[:].unsqueeze(1), rec[:, bass.ds(u, 1), :], 1.0).then_inc(S.sem, 1)
                own("cur")
                v.tensor_copy(cidx[:], cur[:, 12:13]).then_inc(S.sem, 1)
                v.memset(winner[:], -1.0).then_inc(S.sem, 1)
                own("blank")
                dve.wait_ge(O2_pool.sem, O2_pool.after(u, "first"))
                dve.wait_ge(b_own, 16 * (u + 1))
                v.scalar_tensor_tensor(cur[:, 10:11], winner[:], cur[:, 11:12], cur[:, 10:11], ALU.is_equal,
                                       ALU.mult).then_inc(S.sem, 1)
                own("keep")
                v.tensor_scalar_mul(rec[:, bass.ds(u, 1), :], cur[:].unsqueeze(1), 1.0).then_inc(S.sem, 1)
                own("rec")
                v.memset(wv[:, 3:4], 0.0).then_inc(S.sem, 1)

            def loop_b(u):
                S = B_dve

                def own(step):
                    dve.wait_ge(S.sem, S.after(u, step))

                v.tensor_scalar_mul(as_slot(cur, u), at(rec, u), 1.0).then_inc(S.sem, 1)
                own("cur")
                v.tensor_scalar_max(curi[:], cur[:, 0:2], 0.0).then_inc(S.sem, 1)
                v.tensor_scalar(wide, iota[:], cur[:, 0:1], None, ALU.is_equal).then_inc(S.sem, 1)
                own("hot")
                dve.wait_ge(b_m, 16 * (u + 1))
                dve.wait_ge(B_pool.sem, B_pool.after(u, "first"))
                v.tensor_scalar_max(mg[:], mg[:], SELF).then_inc(S.sem, 1)
                own("mx")
                v.tensor_tensor(attv[:, 2, :], cur[:, 2:10], mg[:], ALU.subtract).then_inc(S.sem, 1)
                own("d")
                v.tensor_scalar_min(attv[:, 0, :], attv[:, 2, :], 0.0).then_inc(S.sem, 1)
                dve.wait_ge(B_act.sem, B_act.after(u, "exp"))
                v.tensor_scalar(curS[:, 0:H0], attv[:, 1, :], cur[:, 10:11], None, ALU.mult).then_inc(S.sem, 1)
                v.tensor_copy(curS[:, H0:H0 + 1], cur[:, 10:11]).then_inc(S.sem, 1)
                own("one")
                v.tensor_scalar_mul(at(recS, u), as_slot(curS, u), 1.0).then_inc(S.sem, 1)
                dve.wait_ge(B_pe.sem, B_pe.after(u, "sum"))
                v.tensor_tensor(racc[:], racc[:], ps[:, 0, 0:9 * NB].rearrange("p (b k) -> p b k", b=NB),
                                ALU.add).then_inc(S.sem, 1)
                own("add")
                v.memset(wv[:, 3:4], 0.0).then_inc(S.sem, 1)

            def loop_c(u):
                S = C_dve

                def own(step):
                    dve.wait_ge(S.sem, S.after(u, step))

                v.tensor_scalar_mul(as_slot(cur, u), at(rec, u), 1.0).then_inc(S.sem, 1)
                v.tensor_scalar_mul(as_slot(curS, u), at(recS, u), 1.0).then_inc(S.sem, 1)
                own("curS")
                v.tensor_scalar_max(curi[:], cur[:, 0:2], 0.0).then_inc(S.sem, 1)
                v.tensor_scalar(wide, iota[:], cur[:, 0:1], None, ALU.is_equal).then_inc(S.sem, 1)
                dve.wait_ge(c_gather, 32 * (u + 1))
                dve.wait_ge(C_pool.sem, C_pool.after(u, "first"))
                v.tensor_tensor(attv[:, 0, :], curS[:, 0:H0], tg[:, 0:H0], ALU.mult).then_inc(S.sem, 1)
                own("sp")
                v.tensor_reduce(wv[:, 0:1], attv[:, 0, :], X, ALU.add).then_inc(S.sem, 1)
                v.tensor_tensor(wv[:, 1:2], curS[:, H0:H0 + 1], tg[:, H0:H0 + 1], ALU.mult).then_inc(S.sem, 1)
                own("nb")
                v.tensor_tensor(wv[:, 2:3], wv[:, 0:1], wv[:, 1:2], ALU.subtract).then_inc(S.sem, 1)
                own("w")
                v.tensor_scalar(xso[:, 0, :], xso[:, 1, :], wv[:, 2:3], None, ALU.mult).then_inc(S.sem, 1)
                for b in range(NB):
                    dve.wait_ge(C_pe.sem, C_pe.after(u, f"corr{b}"))
                    v.tensor_tensor(ax[:, b, :], ax[:, b, :], bank(b % 8), ALU.add).then_inc(S.sem, 1)
                own(f"add{NB - 1}")
                v.memset(wv[:, 3:4], 0.0).then_inc(S.sem, 1)

            count = how_many(dve)
            tiles(dve, loop_a, count)
            v.tensor_copy(rt[:, 3], mrow[:]).then_inc(m_made, 1)
            with dve.If(P < count):
                v.memset(wide, 0.0).then_inc(owner_zero, 1)
                every_tile(dve, loop_put, count)
                every_tile(dve, loop_get, count)
            tiles(dve, loop_b, count)

            v.tensor_scalar_max(rt[:, 0], mrow[:], SELF).then_inc(mx_made, 1)
            link(v.tensor_tensor(selfw[:, 0, :], deg[:, 0, :], deg[:, 1, :], ALU.subtract))
            link(v.tensor_tensor(selfw[:, 1, :], selfw[:, 0, :], racc[:, :, H0], ALU.subtract))
            dve.wait_ge(e_made, 2)
            link(v.tensor_tensor(rt[:, 3], rt[:, 1], selfw[:, 1, :].unsqueeze(2).to_broadcast([P, NB, H0]), ALU.mult))
            link(v.tensor_tensor(rt[:, 3], rt[:, 3], rt[:, 2], ALU.add))
            link(v.tensor_tensor(rt[:, 3], rt[:, 3], racc[:, :, 0:H0], ALU.add))
            link(v.reciprocal(rt[:, 0], rt[:, 3]))
            link(v.tensor_scalar_mul(tab[:, :, 0:H0], rt[:, 0], 1.0 / H0))
            link(v.tensor_tensor(rt[:, 3], rt[:, 1], tab[:, :, 0:H0], ALU.mult))
            v.tensor_reduce(tab[:, :, H0:H0 + 1], rt[:, 3], X, ALU.add).then_inc(w_made, 1)
            link(v.tensor_tensor(rt[:, 0], rt[:, 2], tab[:, :, 0:H0], ALU.mult))
            dve.wait_ge(w_made, 1)
            link(v.tensor_reduce(selfw[:, 0, :], rt[:, 0], X, ALU.add))
            link(v.tensor_tensor(selfw[:, 1, :], tab[:, :, H0], deg[:, 1, :], ALU.mult))
            link(v.tensor_tensor(selfw[:, 0, :], selfw[:, 0, :], selfw[:, 1, :], ALU.subtract))
            v.tensor_scalar_add(selfw[:, 1, :], selfw[:, 0, :], 1.0).then_inc(sw_made, 1)
            for b in range(NB):
                dve.wait_ge(scaled, b + 1)
                link(v.scalar_tensor_tensor(ax[:, b, :], ax[:, b, :], tab[:, b, H0:H0 + 1], x_again[:, b, :],
                                            ALU.mult, ALU.add))
            dve.wait_ge(l1_load, 64)
            for k in range(2):
                link(v.tensor_tensor(wtmp.rearrange("p k h d -> p (k h) d"),
                                     Wseq.rearrange("p k (h d) -> p (k h) d", h=H1),
                                     a12[:, k, :].unsqueeze(1).to_broadcast([P, KT * H1, D1]), ALU.mult))
                v.tensor_reduce(Wa[:, :, k, :], wtmp, X, ALU.add).then_inc(wa_made, 1)
                dve.wait_ge(wa_made, k + 1)
            tiles(dve, loop_c, count)

            def measure_rows(b):
                link(v.bn_stats(stats[:, b, :], x1[:, b, :]))
                v.bn_aggr(mv[:, b, :], stats[:, b, :]).then_inc(var_made, 1)

            def normalize(done, layer):
                dve.wait_ge(root_made, layer + 1)
                link(v.reciprocal(rstd[:, 1, :], rstd[:, 0, :]))
                for b in range(NB):
                    v.tensor_scalar(x1[:, b, :], x1[:, b, :], mv[:, b, 0:1], rstd[:, 1, b:b + 1], ALU.subtract,
                                    ALU.mult).then_inc(done, 1)

            def add_elu(b):
                dve.wait_ge(z_exp, b + 1)
                link(v.scalar_tensor_tensor(zt2[:, b % 2, :], bank(6 + b % 2), 0.0, ze[:, b % 2, :], ALU.max, ALU.add))
                v.scalar_tensor_tensor(x1[:, b, :], zt2[:, b % 2, :], -1.0, x1[:, b, :], ALU.add,
                                       ALU.add).then_inc(z_used, 1)
                dve.wait_ge(z_used, b + 1)
                measure_rows(b)

            for b in range(NB):
                measure_rows(b)
            normalize(x1_made, 0)

            for b in range(NB):
                dve.wait_ge(seq_made, b + 1)
                v.tensor_copy(seq[:, b, :], bank(2 + b % 2)).then_inc(seq_saved, 1)
                v.tensor_copy(s12[:, b].rearrange("p s h -> p (s h)"), ps[:, 4 + b % 2, 0:2 * H1]).then_inc(seq_saved, 1)
                list_edges(b)
            dve.wait_ge(seq_saved, 2 * NB)
            v.tensor_reduce(gm[:, 0, :], s12[:, :, 1, :].rearrange("p b h -> p h b"), X, ALU.max).then_inc(g_part, 1)
            dve.wait_ge(g_turned, 1)
            link(v.tensor_reduce(gm[0:H1, 2, 0:1], ps[0:H1, 6, 0:P], X, ALU.max))
            v.tensor_scalar(gm[0:H1, 1, :], ident[0:H1, 0:H1], gm[0:H1, 2, 0:1], None, ALU.mult).then_inc(g_diag, 1)
            dve.wait_ge(g_all, 1)
            link(v.tensor_copy(M2[:], ps[:, 7, 0:H1]))
            mB = M2[:].unsqueeze(1).to_broadcast([P, NB, H1])
            def tie(ins):
                ties[0] += 1
                ins.then_inc(e_link, 1)
                dve.wait_ge(e_link, ties[0])

            ties = [0]

            def make_span(b):
                if b >= 2:
                    dve.wait_ge(e_spread, b - 1)
                v.tensor_scalar(espan[:, b % 2], iota[:, 0:KE * P], eend[:, 1, b:b + 1], None,
                                ALU.is_lt).then_inc(sp_half, 1)
                dve.wait_ge(sp_half, b + 1)
                v.scalar_tensor_tensor(espan[:, b % 2], iota[:, 0:KE * P], eend[:, 0, b:b + 1], espan[:, b % 2],
                                       ALU.is_ge, ALU.mult).then_inc(e_span, 1)

            def finish(b):
                dve.wait_ge(e_agg, b + 1)
                v.reciprocal(sden[:, b % 2], ps[:, b % 2, DEN:DEN + H1]).then_inc(e_rec, 1)
                dve.wait_ge(e_rec, b + 1)
                v.tensor_tensor(hid[:, b, :].rearrange("p (h d) -> p h d", h=H1),
                                bank(2 + b % 2).rearrange("p (h d) -> p h d", h=H1),
                                sden[:, b % 2].unsqueeze(2).to_broadcast([P, H1, D1]), ALU.mult).then_inc(e_hid, 1)

            def sparse():
                v.tensor_copy(sc[:, :, 0, :], s12[:, :, 0, :]).then_inc(pre_sc, 1)
                v.tensor_tensor(EF[:, 0], s12[:, :, 0, :], mB, ALU.add).then_inc(pre_sc, 1)
                dve.wait_ge(pre_sc, 2)
                v.scalar_tensor_tensor(sc[:, :, 1, :], EF[:, 0], SLOPE, EF[:, 0], ALU.mult, ALU.max).then_inc(sc_made, 1)
                dve.wait_ge(seq_made, NB)
                make_span(0)
                dve.wait_ge(tab_store, 32 * NB)
                for b in range(NB):
                    if b + 1 < NB:
                        make_span(b + 1)
                    dve.wait_ge(e_spread, b + 1)
                    dve.wait_ge(e_gather[b % GR], 16 * KE * (b // GR + 1))
                    rows = ps[:, b % 2, 0:KE * 2 * H1].rearrange("p (k s h) -> p k s h", k=KE, s=2)
                    a0, a1_, a2_ = (earg[:, n].rearrange("p (k h) -> p k h", k=KE) for n in range(3))
                    if b >= 1:
                        dve.wait_ge(e_exp, b)
                    v.tensor_tensor(a0, rows[:, :, 0, :], G[:, b % GR, :, D:D + H1], ALU.add).then_inc(sp_arg, 1)
                    dve.wait_ge(sp_arg, 4 * b + 1)
                    v.scalar_tensor_tensor(a1_, a0, SLOPE, a0, ALU.mult, ALU.max).then_inc(sp_arg, 1)
                    dve.wait_ge(sp_arg, 4 * b + 2)
                    v.tensor_tensor(a0, a1_, rows[:, :, 1, :], ALU.subtract).then_inc(sp_arg, 1)
                    dve.wait_ge(sp_arg, 4 * b + 3)
                    v.tensor_scalar_min(a2_, a0, 0.0).then_inc(e_arg, 1)
                    for k in range(KE):
                        v.tensor_scalar(ehot[:, b % 2, k, :], iota[:, 0:P], erow[:, b * KE + k:b * KE + k + 1], None,
                                        ALU.is_equal)
                    dve.wait_ge(e_exp, b + 1)
                    v.memset(wv[:, 3:4], 0.0).then_inc(sp_arg, 1)
                    for k in range(KE):
                        g3 = G[:, b % GR, k, 0:D].rearrange("p (h d) -> p h d", h=H1)
                        v.tensor_tensor(g3, g3, G[:, b % GR, k, D:D + H1].unsqueeze(2).to_broadcast([P, H1, D1]),
                                        ALU.mult).then_inc(e_mul, 1)
                    if b >= 1:
                        finish(b - 1)
                    if b >= 4:
                        add_elu(b - 4)
                finish(NB - 1)
                for b in range(NB - 4, NB):
                    add_elu(b)

            def dense():
                tie(v.tensor_tensor(EF[:, 0], s12[:, :, 0, :], mB, ALU.add))
                tie(v.scalar_tensor_tensor(EF[:, 1], EF[:, 0], SLOPE, EF[:, 0], ALU.mult, ALU.max))
                tie(v.tensor_tensor(z[:, 0], EF[:, 0], EF[:, 1], ALU.subtract))
                v.scalar_tensor_tensor(z[:, 1], EF[:, 0], SLOPE, EF[:, 1], ALU.mult, ALU.subtract).then_inc(args_made, 1)
                dve.wait_ge(exps_made, 1)
                v.tensor_tensor(z[:, 0], s12[:, :, 1, :], mB, ALU.subtract).then_inc(args_made, 1)
                dve.wait_ge(exps_made, 4)
                dve.wait_ge(s1_store, 32)
                tie(v.memset(seqh[:, :, D1:D1 + 1], 1.0))
                with dve.Fori(0, H1) as h:
                    L = L_dve

                    def own(step):
                        dve.wait_ge(L.sem, L.after(h, step))

                    v.tensor_scalar_mul(seqh[:, :, 0:D1], seq[:, :, bass.ds(h * D1, D1)], 1.0).then_inc(L.sem, 1)
                    v.tensor_scalar_mul(Fh[:].unsqueeze(3), EF[:, 2:4, :, bass.ds(h, 1)], 1.0).then_inc(L.sem, 1)
                    own("Fh")
                    dve.wait_ge(c_eb, 32 * (h + 1))
                    for j in range(NB):
                        v.tensor_scalar(p_raw, eB[:, 0, :], Fh[:, 0, j:j + 1], None, ALU.mult).then_inc(L.sem, 1)
                        own(f"t1_{j}")
                        v.scalar_tensor_tensor(p_raw, eB[:, 1, :], Fh[:, 1, j:j + 1], p_raw, ALU.mult,
                                               ALU.max).then_inc(L.sem, 1)
                        own(f"t2_{j}")
                        if j >= 2:
                            dve.wait_ge(L_pe.sem, L_pe.after(h, f"j{j - 2}"))
                        v.tensor_tensor(p_buf[:, j % 2, :], p_raw, adjT[:, j, :], ALU.mult).then_inc(L.sem, 1)
                        own(f"p_{j}")
                    dve.wait_ge(L_pe.sem, L_pe.after(h, f"j{NB - 1}"))
                    O = ps[:, 0:2, 0:8 * (D1 + 1)].rearrange("p a (b d) -> p a b d", b=8)
                    v.reciprocal(rden[:].unsqueeze(3), O[:, :, :, D1:D1 + 1]).then_inc(L.sem, 1)
                    own("rd")
                    for a in range(2):
                        ins = v.tensor_tensor(hid[:, 8 * a:8 * a + 8, bass.ds(h * D1, D1)], O[:, a, :, 0:D1],
                                              rden[:, a, :].unsqueeze(2).to_broadcast([P, 8, D1]), ALU.mult)
                    ins.then_inc(L.sem, 1)
                    own("hid")
                    v.memset(wv[:, 3:4], 0.0).then_inc(L.sem, 1)

            misfit = misfits(dve)
            both = links[0]
            with dve.If(misfit < 1):
                sparse()
            one_end, links[0] = links[0], both
            with dve.If(0 < misfit):
                dense()
                for b in range(NB):
                    add_elu(b)
            assert links[0] == one_end
            normalize(fin, 1)


_INS = ['x', 'adj', 'L0_gnn_rel_pair_index', 'L0_gnn_Wq', 'L0_gnn_bq', 'L0_gnn_Wk', 'L0_gnn_bk', 'L1_gnn_W_seq',
        'L1_gnn_a1', 'L1_gnn_a2', 'L1_gnn_W_out', 'L1_gnn_b_out']
_OUTS = [((2048, 512), 'float32')]


def kernel(**inputs):
    import numpy as _np
    import concourse.bacc as _bacc
    from concourse import mybir as _mybir
    from concourse.bass_utils import run_bass_kernel_spmd as _run

    nc = _bacc.Bacc("TRN2", target_bir_lowering=False, num_devices=1)
    arrays, args = {}, []
    for name in _INS:
        a = _np.ascontiguousarray(inputs[name])
        arrays[f"in_{name}_dram"] = a
        args.append(nc.dram_tensor(f"in_{name}_dram", a.shape, _mybir.dt.from_np(a.dtype), kind="ExternalInput").ap())
    for i, (shape, dtype) in enumerate(_OUTS):
        dt = _mybir.dt.from_np(_np.dtype(dtype))
        args.append(nc.dram_tensor(f"out_{i}_dram", shape, dt, kind="ExternalOutput").ap())
    two_layer_graph_attention(nc, *args)
    r = _run(nc, [arrays], core_ids=[0])
    got = tuple(r.results[0][f"out_{i}_dram"] for i in range(len(_OUTS)))
    return got[0]
```
